# Optimizing a Trainium2 kernel written in Bass

```python
import numpy as np
import jax
import jax.numpy as jnp

def _softmax(x, axis=-1):
    return jax.nn.softmax(x, axis=axis)

def _gelu(x):
    return jax.nn.gelu(x, approximate=True)

def _silu(x):
    return jax.nn.silu(x)

def _sigmoid(x):
    return jax.nn.sigmoid(x)

def _layernorm(x, axis=-1, eps=1e-05):
    m = jnp.mean(x, axis=axis, keepdims=True)
    v = jnp.var(x, axis=axis, keepdims=True)
    return (x - m) / jnp.sqrt(v + eps)

def _scatter_add(tgt, idx, src, axis=0):
    return tgt.at[idx].add(src)

def _segment_sum(src, seg, n):
    return jax.ops.segment_sum(src, seg, n)
kernel_name = 'mk_adj_ffn_d1_adj_r2_d910b6'

def setup_inputs(seed: int=0):
    np.random.seed(seed)
    _w = jnp.asarray

    def _rec_inputs():
        import jax
        import jax.numpy as jnp
        _gk = jax.random.key(seed)
        x = -0.0003929 + 0.9999 * jax.random.normal(jax.random.fold_in(_gk, 1), (64, 128, 128), jnp.float32)
        _a = jax.random.bernoulli(jax.random.fold_in(_gk, 2), 0.015625, (64, 128, 128))
        _af = _a.astype(jnp.float32)
        adj = _af
        return (x, adj)
    x, adj = _rec_inputs()

    def _L0_gnn_setup():
        import jax, jax.numpy as jnp
        import numpy as np
        NEG = 9000000000000000.0
        key = jax.random.key(seed)
        ks = jax.random.split(key, 7)
        B, N, DIN, H, DOUT = (128, 256, 128, 128, 128)
        x = jax.random.normal(ks[0], (B, N, DIN), dtype=jnp.float32)
        mask = (jax.random.uniform(ks[1], (B, N, N)) > 0.5).astype(jnp.float32)

        def lin(k, fan_in, fan_out):
            kw, kb = jax.random.split(k)
            bound = 1.0 / np.sqrt(fan_in)
            W = jax.random.uniform(kw, (fan_in, fan_out), minval=-bound, maxval=bound, dtype=jnp.float32)
            b = jax.random.uniform(kb, (fan_out,), minval=-bound, maxval=bound, dtype=jnp.float32)
            return (W, b)
        Wv, bv = lin(ks[2], DIN, H)
        Wk, bk = lin(ks[3], DIN, H)
        Wq, bq = lin(ks[4], DIN, H)
        Wo, bo = lin(ks[5], H, DOUT)
        return {'x': x, 'mask': mask, 'Wv': Wv, 'bv': bv, 'Wk': Wk, 'bk': bk, 'Wq': Wq, 'bq': bq, 'Wo': Wo, 'bo': bo}
    _L0_gnn_all = _L0_gnn_setup()
    _L0_gnn_in = {k: v for k, v in _L0_gnn_all.items() if k in ('Wv', 'bv', 'Wk', 'bk', 'Wq', 'bq', 'Wo', 'bo')}
    del _L0_gnn_all

    def _L0_ffn_setup():
        import math
        import jax, jax.numpy as jnp
        import numpy as np
        CAPACITY_FACTOR = 1.25
        TOP_K = 2
        LN_EPS = 1e-05

        def _layer_norm(x, gamma, beta):
            mu = jnp.mean(x, axis=-1, keepdims=True)
            var = jnp.var(x, axis=-1, keepdims=True)
            return (x - mu) * jax.lax.rsqrt(var + LN_EPS) * gamma + beta
        key = jax.random.key(seed)
        ks = jax.random.split(key, 4)
        B, S, D, F, E = (8, 2048, 128, 256, 8)
        x = jax.random.normal(ks[0], (B, S, D), dtype=jnp.float32)
        Wr = jax.random.normal(ks[1], (D, E), dtype=jnp.float32) / np.sqrt(D)
        br = jnp.zeros((E,), jnp.float32)
        W1 = jax.random.normal(ks[2], (E, D, F), dtype=jnp.float32) / np.sqrt(D)
        b1 = jnp.zeros((E, F), jnp.float32)
        W2 = jax.random.normal(ks[3], (E, F, D), dtype=jnp.float32) / np.sqrt(F)
        b2 = jnp.zeros((E, D), jnp.float32)
        gamma = jnp.ones((D,), jnp.float32)
        beta = jnp.zeros((D,), jnp.float32)
        return {'x': x, 'Wr': Wr, 'br': br, 'W1': W1, 'b1': b1, 'W2': W2, 'b2': b2, 'gamma': gamma, 'beta': beta}
    _L0_ffn_all = _L0_ffn_setup()
    _L0_ffn_in = {k: v for k, v in _L0_ffn_all.items() if k in ('Wr', 'br', 'W1', 'b1', 'W2', 'b2', 'gamma', 'beta')}
    del _L0_ffn_all
    return {'x': x, 'adj': adj, 'L0_gnn_Wv': _L0_gnn_in['Wv'], 'L0_gnn_bv': _L0_gnn_in['bv'], 'L0_gnn_Wk': _L0_gnn_in['Wk'], 'L0_gnn_bk': _L0_gnn_in['bk'], 'L0_gnn_Wq': _L0_gnn_in['Wq'], 'L0_gnn_bq': _L0_gnn_in['bq'], 'L0_gnn_Wo': _L0_gnn_in['Wo'], 'L0_gnn_bo': _L0_gnn_in['bo'], 'L0_ffn_Wr': _L0_ffn_in['Wr'], 'L0_ffn_br': _L0_ffn_in['br'], 'L0_ffn_W1': _L0_ffn_in['W1'], 'L0_ffn_b1': _L0_ffn_in['b1'], 'L0_ffn_W2': _L0_ffn_in['W2'], 'L0_ffn_b2': _L0_ffn_in['b2'], 'L0_ffn_gamma': _L0_ffn_in['gamma'], 'L0_ffn_beta': _L0_ffn_in['beta']}

def reference(x, adj, L0_gnn_Wv, L0_gnn_bv, L0_gnn_Wk, L0_gnn_bk, L0_gnn_Wq, L0_gnn_bq, L0_gnn_Wo, L0_gnn_bo, L0_ffn_Wr, L0_ffn_br, L0_ffn_W1, L0_ffn_b1, L0_ffn_W2, L0_ffn_b2, L0_ffn_gamma, L0_ffn_beta):
    import jax
    import jax.numpy as jnp

    def _L0_gnn_ref(x, mask, Wv, bv, Wk, bk, Wq, bq, Wo, bo):
        import jax, jax.numpy as jnp
        import numpy as np
        NEG = 9000000000000000.0
        v = jax.nn.relu(jnp.einsum('bnd,dh->bnh', x, Wv) + bv)
        q = jax.nn.relu(jnp.einsum('bnd,dh->bnh', x, Wq) + bq)
        k = jax.nn.relu(jnp.einsum('bnd,dh->bnh', x, Wk) + bk)
        scores = jnp.einsum('bnh,bmh->bnm', q, k)
        att = jax.nn.softmax(scores * mask - NEG * (1.0 - mask), axis=2)
        out = jnp.einsum('bnm,bmh->bnh', att, v)
        out = jax.nn.relu(jnp.einsum('bnh,ho->bno', out, Wo) + bo)
        return out

    def _L0_ffn_ref(x, Wr, br, W1, b1, W2, b2, gamma, beta):
        import math
        import jax, jax.numpy as jnp
        import numpy as np
        CAPACITY_FACTOR = 1.25
        TOP_K = 2
        LN_EPS = 1e-05

        def _layer_norm(x, gamma, beta):
            mu = jnp.mean(x, axis=-1, keepdims=True)
            var = jnp.var(x, axis=-1, keepdims=True)
            return (x - mu) * jax.lax.rsqrt(var + LN_EPS) * gamma + beta
        B, S, D = x.shape
        E = Wr.shape[1]
        N = B * S
        K = TOP_K
        logits = jnp.mean(x, axis=1) @ Wr + br
        routing_weights = jax.nn.softmax(logits, axis=-1)
        capacity = float(math.ceil(N * CAPACITY_FACTOR / E))
        expected_loads = routing_weights.sum(axis=0) * (N / B)
        scale = jnp.where(expected_loads > capacity, capacity / expected_loads, 1.0)
        routing_weights = jax.nn.softmax(routing_weights * scale, axis=-1)
        rw_tok = jnp.broadcast_to(routing_weights[:, None, :], (B, S, E)).reshape(N, E)
        top_w, top_i = jax.lax.top_k(rw_tok, K)
        top_w = jax.nn.softmax(top_w, axis=-1)
        xf = x.reshape(N, D)
        h = jax.nn.gelu(jnp.einsum('nd,edf->enf', xf, W1) + b1[:, None, :], approximate=False)
        y = jnp.einsum('enf,efd->end', h, W2) + b2[:, None, :]
        w_dense = jnp.zeros((N, E), x.dtype).at[jnp.arange(N)[:, None], top_i].add(top_w)
        out = jnp.einsum('ne,end->nd', w_dense, y).reshape(B, S, D)
        out = _layer_norm(out + x, gamma, beta)
        return out
    x = x + _L0_gnn_ref(_layernorm(x, axis=-1), adj, L0_gnn_Wv, L0_gnn_bv, L0_gnn_Wk, L0_gnn_bk, L0_gnn_Wq, L0_gnn_bq, L0_gnn_Wo, L0_gnn_bo)
    x = x + _L0_ffn_ref(_layernorm(x, axis=-1), L0_ffn_Wr, L0_ffn_br, L0_ffn_W1, L0_ffn_b1, L0_ffn_W2, L0_ffn_b2, L0_ffn_gamma, L0_ffn_beta)
    return x

_drawn_inputs = setup_inputs


def setup_inputs(seed=0):
    import zlib

    import numpy as np

    out = dict(_drawn_inputs(seed))
    spreads = {'L0_ffn_br': (0.0, 0.1),
     'L0_ffn_b1': (0.0, 0.375),
     'L0_ffn_b2': (0.0, 0.268),
     'L0_ffn_gamma': (1.0, 0.2),
     'L0_ffn_beta': (0.0, 0.1)}
    factors = {'L0_gnn_bk': 8.0, 'L0_gnn_bq': 8.0}
    for name, (base, spread) in spreads.items():
        noise = np.random.default_rng([zlib.crc32(name.encode()), seed]).standard_normal(out[name].shape)
        drawn = base * np.exp(spread * noise) if base else spread * noise
        out[name] = jnp.asarray(drawn.astype(out[name].dtype))
    for name, factor in factors.items():
        out[name] = (out[name] * factor).astype(out[name].dtype)
    return out
```

```python
from contextlib import ExitStack

import concourse.bass as bass
from concourse import mybir

F32 = mybir.dt.float32
I32 = mybir.dt.int32
U32 = mybir.dt.uint32
ALU = mybir.AluOpType
ACT = mybir.ActivationFunctionType
AX = mybir.AxisListType

P = 128
G = 4
TOP = 2
NEG = 9000000000000000.0
LN_EPS = 1e-5
RSQRT_MAGIC = float(0x5F3759DF)
NEWTONS = 3
CHAIN = 3 + 3 * NEWTONS
CAPACITY_FACTOR = 1.25


def wait(engine, semaphore, value):
    if not isinstance(value, int) or value > 0:
        engine.wait_ge(semaphore, value)


def after(engine, semaphore, i):
    if not isinstance(i, int):
        engine.wait_ge(semaphore, 1)


def run_steps(engine, body, first, loop_from, loop_to, end):
    for s in range(first, loop_from):
        body(0, s)
    with engine.Fori(loop_from // 2, loop_to // 2) as i:
        body(i, 0)
        body(i, 1)
    for s in range(loop_to, end):
        body(0, s)


def build(nc, x, adj, Wv, bv, Wk, bk, Wq, bq, Wo, bo, Wr, br, W1, b1, W2, b2, gamma, beta, out):
    GRAPHS, NODES, D = x.shape
    E, _, FF = W1.shape
    FC = FF // P
    GROUPS = GRAPHS // G
    GD = G * D
    W1C = FF + FC
    CAPACITY = float(-(-GRAPHS * NODES * CAPACITY_FACTOR // E))
    assert NODES == P and D == P and FF % P == 0 and GRAPHS % (2 * G) == 0

    def live(g):
        return not isinstance(g, int) or 0 <= g < GROUPS

    bias2_dram = nc.dram_tensor("bias2_scratch", (GRAPHS, D), F32).ap()

    ctx = ExitStack()
    with ctx:
        def sb(name, shape, dt=F32):
            return ctx.enter_context(nc.sbuf_tensor(name, shape, dt))

        def bank(name):
            return ctx.enter_context(nc.psum_tensor(name, [P, GD], F32))

        def sem(name):
            return ctx.enter_context(nc.semaphore(name))

        x_res = sb("x_res", [P, GRAPHS * D])
        xl_res = sb("xl_res", [P, GRAPHS * D])
        xlT_res = sb("xlT_res", [P, GRAPHS * P])
        b2bc = sb("b2bc", [P, GRAPHS * D])
        w1_sb = sb("w1_sb", [P, E * W1C])
        w1v = w1_sb[:, :].rearrange("p (e c) -> p e c", e=E)
        w2_sb = sb("w2_sb", [P, E * FC * D])
        wq_sb, wk_sb, wv_sb, wo_sb = (sb(n, [P, D]) for n in ("wq_sb", "wk_sb", "wv_sb", "wo_sb"))
        wr_sb = sb("wr_sb", [P, E])
        bo_bc = sb("bo_bc", [P, D])
        gamma_bc = sb("gamma_bc", [P, D])
        beta_bc = sb("beta_bc", [P, D])
        br_bc = sb("br_bc", [GRAPHS, E])
        b2_sb = sb("b2_sb", [E, D])
        NROWS = 3 + E * FC
        bias_rows = sb("bias_rows", [NROWS, P])
        bias_cols = sb("bias_cols", [P, 3])
        ident = sb("ident", [P, P])
        ones = sb("ones", [P, W1C])

        adj_sb = sb("adj_sb", [P, 2, GD])
        xn = sb("xn", [P, 2, GD])
        xnT = sb("xnT", [P, GD])
        qT = sb("qT", [P, GD])
        kT = sb("kT", [P, GD])
        vT = sb("vT", [P, GD])
        vw = sb("vw", [P, 2, GD])
        neg_mask = sb("neg_mask", [P, GD])
        score = sb("score", [P, GD])
        prob = sb("prob", [P, GD])
        probT = sb("probT", [P, GD])
        rel = sb("rel", [P, GD])
        xl = sb("xl", [P, 2, GD])
        neg_max = sb("neg_max", [P, 2, G])
        den = sb("den", [P, 2, G])
        rden = sb("rden", [P, 2, G])
        mean_sum = sb("mean_sum", [P, GRAPHS])
        stats = sb("stats", [P, 2, 2 * G, 6])
        mv = sb("mv", [P, 2, 2 * G, 2])
        neg_mean = sb("neg_mean", [P, 2, 2 * G])
        rstd = sb("rstd", [P, 2, 2 * G])
        var_eps = sb("var_eps", [P, 2 * G])
        halved = sb("halved", [P, 2 * G], I32)
        guess = sb("guess", [P, 2 * G], I32)
        newton_y = sb("newton_y", [P, 2 * G])
        newton_t = sb("newton_t", [P, 2 * G])

        rt = sb("rt", [GRAPHS, 16, E])
        r1 = sb("r1", [GRAPHS, 16])
        top_at = sb("top_at", [GRAPHS, E], U32)
        picked = sb("picked", [GRAPHS, 2 * TOP])
        picked_diag = sb("picked_diag", [GRAPHS, 2 * TOP, GRAPHS])
        w_bc = sb("w_bc", [P, TOP, GRAPHS])
        expert = sb("expert", [1, GRAPHS, TOP], I32)
        iota_e = sb("iota_e", [GRAPHS, E])
        denseT = sb("denseT", [E, GRAPHS])
        bias2 = sb("bias2", [GRAPHS, D])

        w1_pick = sb("w1_pick", [P, 2, TOP, W1C])
        hT = sb("hT", [P, 2, TOP * FC * P])
        neg_mr = sb("neg_mr", [P, G])

        b_p, b_t, b_s, b_y, b_q, b_k, b_v, b_w = (bank("bank_" + n) for n in "ptsyqkvw")
        y_banks = (b_v, b_w, b_s, b_t)

        x_in = [sem(f"x_in{n}") for n in range(2)]
        adj_in = [sem(f"adj_in{n}") for n in range(2)]
        gnn_w_in, rows_in, late_w_in, w1_in, w2_in = (
            sem(n) for n in ("gnn_w_in", "rows_in", "late_w_in", "w1_in", "w2_in"))
        zeroed, ident_ready, const_ready = sem("zeroed"), sem("ident_ready"), sem("const_ready")
        cols_in_psum, cols_ready = sem("cols_in_psum"), sem("cols_ready")
        stats1_done, stats2_done = sem("stats1_done"), sem("stats2_done")
        centred = [sem("xn_centred"), sem("xl_centred")]
        ln_chain, ln_ready = sem("ln_chain"), sem("ln_ready")
        xn_ready, xnT_in_psum, xnT_ready = sem("xn_ready"), sem("xnT_in_psum"), sem("xnT_ready")
        q_in_psum, k_in_psum, v_in_psum = sem("q_in_psum"), sem("k_in_psum"), sem("v_in_psum")
        q_ready, k_ready, v_ready = sem("q_ready"), sem("k_ready"), sem("v_ready")
        vw_in_psum, vw_ready = sem("vw_in_psum"), sem("vw_ready")
        scores_in_psum, scores_masked = sem("scores_in_psum"), sem("scores_masked")
        neg_mask_ready, score_ready, max_ready = (
            sem("neg_mask_ready"), sem("score_ready"), sem("max_ready"))
        prob_ready, probT_in_psum, probT_ready = (
            sem("prob_ready"), sem("probT_in_psum"), sem("probT_ready"))
        rden_ready, y_in_psum, rel_ready, x1_ready = (
            sem("rden_ready"), sem("y_in_psum"), sem("rel_ready"), sem("x1_ready"))
        xl_ready, xlT_in_psum, xlT_ready, mean_done = (
            sem("xl_ready"), sem("xlT_in_psum"), sem("xlT_ready"), sem("mean_done"))
        xl_saved = [sem(f"xl_saved{n}") for n in range(2)]
        route_pe, route_dve, route_act = sem("route_pe"), sem("route_dve"), sem("route_act")
        experts_ready = sem("experts_ready")
        bias2_ready, bias2_out, bias2_in = sem("bias2_ready"), sem("bias2_out"), sem("bias2_in")
        w1_picked, h_in_psum, gelu_done, e_in_psum = (
            sem("w1_picked"), sem("h_in_psum"), sem("gelu_done"), sem("e_in_psum"))
        res_ready = sem("group_res_ready")
        z0_done, z_done, zstats_done = sem("z0_done"), sem("z_done"), sem("zstats_done")
        ln2_chain, ln2_ready, unit_ready = (
            sem("ln2_chain"), sem("group_ln2_ready"), sem("group_unit_ready"))
        scaled, shifted, final_ready, out_done = (
            sem("group_scaled"), sem("group_shifted"), sem("group_final_ready"), sem("out_done"))

        def group(tensor, g):
            return tensor[:, bass.ds(g * GD, GD)]

        def graph(tensor, b):
            return tensor[:, bass.ds(b * D, D)]

        def by_graph(ap):
            return ap.rearrange("p (g n) -> p g n", g=G)

        def repeat(ap, times):
            return ap.unsqueeze(1).broadcast_to([ap.shape[0], times, ap.shape[1]])

        block = ctx.enter_context(nc.Block())

        @block.sync
        def _(sp):
            x_v = x.rearrange("b n d -> n b d")
            adj_v = adj.rearrange("b n m -> n b m")

            def load_x(i):
                for n in range(2):
                    wait(sp, x_in[n], 16 * i)
                    after(sp, x_in[n], i)
                    sp.dma_start(by_graph(group(x_res, 2 * i + n)),
                                 x_v[:, bass.ds((2 * i + n) * G, G), :]).then_inc(x_in[n], 16)

            def load_adj(i):
                for n in range(2):
                    g = 2 * i + n
                    wait(sp, adj_in[n], 16 * i)
                    wait(sp, neg_mask_ready, g - 1)
                    wait(sp, scores_masked, g - 1)
                    after(sp, adj_in[n], i)
                    sp.dma_start(by_graph(adj_sb[:, n, :]),
                                 adj_v[:, bass.ds(g * G, G), :]).then_inc(adj_in[n], 16)

            load_x(0)
            load_adj(0)
            load_x(1)
            load_x(2)
            load_adj(1)
            with sp.Fori(2, GROUPS // 2 - 1) as i:
                load_x(i + 1)
                load_adj(i)
            load_adj(GROUPS // 2 - 1)
            sp.dma_start(w1v[:, :, 0:FF], W1.rearrange("e d f -> d e f")).then_inc(w1_in, 16)
            sp.dma_start(w2_sb[:, :].rearrange("p (e c d) -> p e c d", e=E, c=FC),
                         W2.rearrange("e (c p) d -> p e c d", p=P)).then_inc(w2_in, 16)
            sp.wait_ge(bias2_ready, 1)
            sp.dma_start(bias2_dram, bias2[:, :]).then_inc(bias2_out, 16)
            sp.wait_ge(bias2_out, 16)
            sp.dma_start(b2bc[:, 0:GD], bias2_dram[0:G, :].rearrange("b d -> (b d)").unsqueeze(0)
                         .broadcast_to([P, GD])).then_inc(bias2_in, 16)
            sp.wait_ge(bias2_in, 16)
            sp.dma_start(b2bc[:, GD:], bias2_dram[G:, :].rearrange("b d -> (b d)").unsqueeze(0)
                         .broadcast_to([P, (GROUPS - 1) * GD])).then_inc(bias2_in, 16)
            out_v = out.rearrange("b n d -> n b d")

            def store(g):
                sp.wait_ge(final_ready, g + 1)
                after(sp, final_ready, g)
                sp.dma_start(out_v[:, bass.ds(g * G, G), :],
                             by_graph(group(x_res, g))).then_inc(out_done, 16)

            with sp.Fori(0, GROUPS) as g:
                store(g)
            sp.wait_ge(out_done, 16 * GROUPS)

        @block.gpsimd
        def _(pool):
            nc.gpsimd.memset(ident[:, :], 0.0).then_inc(zeroed, 1)
            nc.gpsimd.memset(ones[:, :], 1.0).then_inc(const_ready, 1)
            nc.gpsimd.iota(iota_e[:, :], pattern=[[1, E]], base=0, channel_multiplier=0,
                           allow_small_or_imprecise_dtypes=True).then_inc(const_ready, 1)
            pool.wait_ge(zeroed, 1)
            nc.gpsimd.affine_select(out=ident[:, :], in_=ident[:, :], compare_op=ALU.not_equal,
                                    fill=1.0, base=0, pattern=[[-1, P]],
                                    channel_multiplier=1).then_inc(ident_ready, 1)

            def normalise(dst, g, par, ln, ready):
                def each(ap):
                    return ap[:, par, ln * G:(ln + 1) * G].unsqueeze(2).broadcast_to([P, G, D])

                nc.gpsimd.tensor_tensor(by_graph(dst), by_graph(group(x_res, g)), each(neg_mean),
                                        ALU.add).then_inc(centred[ln], 1)
                wait(pool, centred[ln], g + 1)
                nc.gpsimd.tensor_tensor(by_graph(dst), by_graph(dst), each(rstd),
                                        ALU.mult).then_inc(ready, 1)

            def step(i, c):
                s = 2 * i + c
                g = s + 1
                if live(g):
                    wait(pool, ln_ready, g + 1)
                    wait(pool, xnT_in_psum, g - 1)
                    normalise(xn[:, (c + 1) % 2, :], g, (c + 1) % 2, 0, xn_ready)
                g = s - 1
                if live(g):
                    wait(pool, scores_masked, g + 1)
                    wait(pool, neg_mask_ready, g + 1)
                    nc.gpsimd.tensor_tensor(score[:, :], score[:, :], neg_mask[:, :],
                                            ALU.add).then_inc(score_ready, 1)
                if live(s):
                    pool.wait_ge(adj_in[c % 2], 16 * (i + c // 2 + 1))
                    wait(pool, score_ready, s)
                g = s - 3
                if live(g):
                    wait(pool, ln_ready, g + 5)
                    wait(pool, xlT_in_psum, g - 1)
                    wait(pool, xl_saved[(c + 1) % 2], 16 * (i + (c - 3) // 2))
                    normalise(xl[:, (c + 1) % 2, :], g, (c + 1) % 2, 1, xl_ready)
                g = s
                if live(g):
                    nc.gpsimd.tensor_scalar(neg_mask[:, :], adj_sb[:, c % 2, :], -1.0, NEG,
                                            ALU.add, ALU.mult).then_inc(neg_mask_ready, 1)

            run_steps(pool, step, -1, 6, 14, GROUPS + 3)

            pool.wait_ge(experts_ready, 1)
            pool.wait_ge(w1_in, 16)
            pool.wait_ge(cols_ready, 2)

            def pick(g, j):
                b = g * G + j
                wait(pool, gelu_done, b - 1)
                for k in range(TOP):
                    e = pool.value_load(expert[0:1, bass.ds(b, 1), k], min_val=0, max_val=E - 1)
                    last = nc.gpsimd.tensor_tensor(w1_pick[:, j % 2, k, :],
                                                   w1_sb[:, bass.ds(e * W1C, W1C)], ones[:, :],
                                                   ALU.mult)
                last.then_inc(w1_picked, 1)

            def residual(g, b2_count):
                pool.wait_ge(bias2_in, b2_count)
                nc.gpsimd.tensor_tensor(group(xl_res, g), group(xl_res, g), group(b2bc, g),
                                        ALU.add).then_inc(res_ready, 1)

            pick(0, 0)
            pick(0, 1)
            for n in range(2):
                pool.wait_ge(xl_saved[n], 16 * (GROUPS // 2))
            residual(0, 16)
            pick(0, 2)
            pick(0, 3)
            with pool.Fori(1, GROUPS) as g:
                pick(g, 0)
                pick(g, 1)
                residual(g, 32)
                pick(g, 2)
                pick(g, 3)

        @block.scalar
        def _(act):
            for dst, src in ((wq_sb, Wq), (wk_sb, Wk), (wv_sb, Wv), (wo_sb, Wo)):
                act.dma_start(dst[:, :], src).then_inc(gnn_w_in, 16)
            act.dma_start(bo_bc[:, :], bo.unsqueeze(0).broadcast_to([P, D])).then_inc(gnn_w_in, 16)
            for n, src in enumerate((bq, bk, bv)):
                act.dma_start(bias_rows[n:n + 1, :], src.unsqueeze(0)).then_inc(rows_in, 16)
            act.dma_start(bias_rows[3:NROWS, :],
                          b1.rearrange("e (c p) -> (e c) p", p=P)).then_inc(rows_in, 16)
            act.dma_start(wr_sb[:, :], Wr).then_inc(late_w_in, 16)
            act.dma_start(br_bc[:, :], br.unsqueeze(0).broadcast_to([GRAPHS, E])).then_inc(late_w_in, 16)
            act.dma_start(b2_sb[:, :], b2).then_inc(late_w_in, 16)
            for dst, src in ((gamma_bc, gamma), (beta_bc, beta)):
                act.dma_start(dst[:, :], src.unsqueeze(0).broadcast_to([P, D])).then_inc(late_w_in, 16)
            act.wait_ge(cols_ready, 1)

            def relu_of(dst, src, n, ready):
                nc.scalar.activation(dst[:, :], src[:, :], ACT.Relu,
                                     bias=bias_cols[:, n:n + 1]).then_inc(ready, 1)

            def step(i, c):
                s = 2 * i + c
                g = s - 2
                if live(g):
                    act.wait_ge(probT_in_psum, g + 1)
                    wait(act, y_in_psum, g)
                    nc.scalar.activation(probT[:, :], b_p[:, :], ACT.Copy).then_inc(probT_ready, 1)
                g = s
                if live(g):
                    act.wait_ge(xnT_in_psum, g + 1)
                    wait(act, v_in_psum, g)
                    nc.scalar.activation(xnT[:, :], b_t[:, :], ACT.Copy).then_inc(xnT_ready, 1)
                g = s - 2
                if live(g):
                    act.wait_ge(y_in_psum, g + 1)
                    act.wait_ge(rden_ready, g + 1)
                    wait(act, x1_ready, g)
                    for j in range(G):
                        last = nc.scalar.activation(rel[:, j * D:(j + 1) * D],
                                                    b_y[:, j * D:(j + 1) * D], ACT.Relu,
                                                    scale=rden[:, c % 2, j:j + 1])
                    last.then_inc(rel_ready, 1)
                g = s
                if live(g):
                    act.wait_ge(q_in_psum, g + 1)
                    wait(act, scores_in_psum, g)
                    relu_of(qT, b_q, 0, q_ready)
                g = s - 1
                if live(g):
                    act.wait_ge(max_ready, g + 1)
                    wait(act, probT_in_psum, g)
                    wait(act, rden_ready, g - 1)
                    for j in range(G):
                        last = nc.scalar.activation(
                            prob[:, j * P:(j + 1) * P], score[:, j * P:(j + 1) * P], ACT.Exp,
                            bias=neg_max[:, (c + 1) % 2, j:j + 1],
                            accum_out=den[:, (c + 1) % 2, j:j + 1])
                    last.then_inc(prob_ready, 1)
                g = s
                if live(g):
                    act.wait_ge(k_in_psum, g + 1)
                    relu_of(kT, b_k, 1, k_ready)
                    act.wait_ge(v_in_psum, g + 1)
                    wait(act, vw_in_psum, g)
                    relu_of(vT, b_v, 2, v_ready)
                g = s - 3
                if live(g):
                    act.wait_ge(xlT_in_psum, g + 1)
                    nc.scalar.activation(group(xlT_res, g), b_p[:, :],
                                         ACT.Copy).then_inc(xlT_ready, 1)
                    act.wait_ge(xl_ready, g + 1)
                    act.dma_start(group(xl_res, g),
                                  xl[:, (c + 1) % 2, :]).then_inc(xl_saved[(c + 1) % 2], 16)

            run_steps(act, step, 0, 4, 16, GROUPS + 3)

            act.wait_ge(route_dve, 2)
            nc.scalar.activation(rt[:, 1, :], rt[:, 0, :], ACT.Exp, bias=r1[:, 0:1],
                                 accum_out=r1[:, 1:2]).then_inc(route_act, 1)
            act.wait_ge(route_dve, 9)
            nc.scalar.activation(rt[:, 5, :], rt[:, 4, :], ACT.Exp, bias=r1[:, 3:4],
                                 accum_out=r1[:, 4:5]).then_inc(route_act, 1)
            act.wait_ge(route_dve, 14)
            nc.scalar.activation(r1[:, 7:8], r1[:, 6:7], ACT.Exp).then_inc(route_act, 1)

            def gelu(g, j):
                b = g * G + j
                act.wait_ge(h_in_psum, b + 1)
                wait(act, e_in_psum, b - 1)
                bh = (b_q, b_k)[j % 2]
                for k in range(TOP):
                    for f in range(FC):
                        at = (k * FC + f) * P
                        last = nc.scalar.activation(
                            hT[:, j % 2, at:at + P], bh[:, at:at + P], ACT.Gelu,
                            bias=w1_pick[:, j % 2, k, FF + f:FF + f + 1])
                last.then_inc(gelu_done, 1)

            def unit(g, j):
                if j == 0:
                    wait(act, ln2_ready, g + 1)
                last = nc.scalar.activation(graph(xl_res, g * G + j), graph(xl_res, g * G + j),
                                            ACT.Identity, scale=rstd[:, 0, j:j + 1],
                                            bias=neg_mr[:, j:j + 1])
                if j == G - 1:
                    last.then_inc(unit_ready, 1)

            def group_step(g, gelus, units):
                for j in range(G):
                    if gelus:
                        gelu(g, j)
                    if units:
                        unit(g - 2, j)

            group_step(0, True, False)
            group_step(1, True, False)
            with act.Fori(2, GROUPS) as g:
                group_step(g, True, True)
            group_step(GROUPS, False, True)
            group_step(GROUPS + 1, False, True)

        @block.vector
        def _(dve):
            dve.wait_ge(cols_in_psum, 1)
            nc.vector.tensor_copy(bias_cols[:, :], b_t[:, 0:3]).then_inc(cols_ready, 1)
            nc.vector.tensor_copy(w1v[:, :, FF:W1C],
                                  b_t[:, 3:NROWS].rearrange("p (e c) -> p e c", e=E)
                                  ).then_inc(cols_ready, 1)

            def rsqrt_op(n, chain, base, lo, hi, dst, ready):
                v, t, y = var_eps[:, lo:hi], newton_t[:, lo:hi], newton_y[:, lo:hi]
                dve.wait_ge(chain, base + n + 1)
                if n == 0:
                    op = nc.vector.tensor_scalar(halved[:, lo:hi], v.bitcast(I32), 1, None,
                                                 ALU.logical_shift_right)
                elif n == 1:
                    op = nc.vector.tensor_scalar(guess[:, lo:hi], halved[:, lo:hi], -1.0,
                                                 RSQRT_MAGIC, ALU.mult, ALU.add)
                else:
                    r, m = divmod(n - 2, 3)
                    prev = guess[:, lo:hi].bitcast(F32) if r == 0 else y
                    if m == 0:
                        op = nc.vector.tensor_tensor(t, prev, prev, ALU.mult)
                    elif m == 1:
                        op = nc.vector.scalar_tensor_tensor(t, t, -0.5, v, ALU.mult, ALU.mult)
                    else:
                        to = dst if r == NEWTONS - 1 else y
                        op = nc.vector.scalar_tensor_tensor(to, t, 1.5, prev, ALU.add, ALU.mult)
                op.then_inc(ready if n == 1 + 3 * NEWTONS else chain, 1)

            RSQRT_OPS = 2 + 3 * NEWTONS

            def step(i, c):
                s = 2 * i + c
                par, odd = c % 2, (c + 1) % 2

                def x_stats(js):
                    g = s + 3
                    if live(g):
                        for j in js:
                            op = nc.vector.bn_stats(stats[:, odd, j, :], graph(x_res, g * G + j))
                            if j == G - 1:
                                op.then_inc(stats1_done, 1)

                g = s - 2
                if live(g):
                    dve.wait_ge(prob_ready, g + 1)
                    wait(dve, rel_ready, g - 1)
                    nc.vector.reciprocal(rden[:, par, :], den[:, par, :]).then_inc(rden_ready, 1)
                if live(s + 3):
                    dve.wait_ge(x_in[odd], 16 * (i + (c + 3) // 2 + 1))
                g = s - 1
                if live(g):
                    dve.wait_ge(adj_in[odd], 16 * (i + (c - 1) // 2 + 1))
                    wait(dve, prob_ready, g)
                    dve.wait_ge(scores_in_psum, g + 1)
                    nc.vector.tensor_tensor(score[:, :], b_s[:, :], adj_sb[:, odd, :],
                                            ALU.mult).then_inc(scores_masked, 1)
                    wait(dve, y_in_psum, g - 1)
                    if isinstance(g, int) and g == 0:
                        dve.wait_ge(gnn_w_in, 16 * 5)
                    dve.wait_ge(vw_in_psum, g + 1)
                    nc.vector.tensor_tensor(by_graph(vw[:, odd, :]), by_graph(b_w[:, :]),
                                            repeat(bo_bc[:, :], G), ALU.add).then_inc(vw_ready, 1)
                x_stats((0, 1))
                g = s - 2
                if live(g):
                    dve.wait_ge(rel_ready, g + 1)
                    nc.vector.tensor_tensor(group(x_res, g), group(x_res, g), rel[:, :],
                                            ALU.add).then_inc(x1_ready, 1)
                    dve.wait_ge(x1_ready, g + 1)
                g = s - 1
                if live(g):
                    wait(dve, prob_ready, g - 1)
                    dve.wait_ge(score_ready, g + 1)
                    nc.vector.tensor_reduce(neg_max[:, odd, :], by_graph(score[:, :]), AX.X,
                                            ALU.max, negate=True).then_inc(max_ready, 1)
                g = s - 2
                if live(g):
                    for j in range(G):
                        op = nc.vector.bn_stats(stats[:, par, G + j, :], graph(x_res, g * G + j))
                    op.then_inc(stats2_done, 1)
                lo, hi = (0 if live(s + 2) else G), (2 * G if live(s - 2) else G)
                chained = live(s + 2) or live(s - 2)
                base = CHAIN * (s + 2)
                if live(s + 2):
                    dve.wait_ge(stats1_done, s + 3)
                    wait(dve, xn_ready, s + 1)
                if live(s - 2):
                    dve.wait_ge(stats2_done, s - 1)
                if chained:
                    wait(dve, xl_ready, s - 3)
                g = s - 4
                if live(g):
                    dve.wait_ge(xlT_ready, g + 1)
                    nc.vector.tensor_reduce(mean_sum[:, bass.ds(g * G, G)],
                                            by_graph(group(xlT_res, g)),
                                            AX.X, ALU.add).then_inc(mean_done, 1)
                if chained:
                    for j in range(lo, hi):
                        op = nc.vector.bn_aggr(mv[:, par, j, :], stats[:, par, j, :])
                    op.then_inc(ln_chain, 1)
                x_stats((2,))
                if chained:
                    dve.wait_ge(ln_chain, base + 1)
                    nc.vector.tensor_scalar(var_eps[:, lo:hi], mv[:, par, lo:hi, 1], LN_EPS, None,
                                            ALU.add).then_inc(ln_chain, 1)
                    nc.vector.tensor_scalar(neg_mean[:, par, lo:hi], mv[:, par, lo:hi, 0], -1.0,
                                            None, ALU.mult)
                x_stats((3,))
                if chained:
                    for n in range(RSQRT_OPS):
                        rsqrt_op(n, ln_chain, base + 1, lo, hi, rstd[:, par, lo:hi], ln_ready)

            run_steps(dve, step, -3, 4, 12, GROUPS + 4)

            count = [0]

            def then(op):
                count[0] += 1
                op.then_inc(route_dve, 1)
                dve.wait_ge(route_dve, count[0])

            def columns(n):
                return r1[:, n:n + 1]

            vec = nc.vector
            dve.wait_ge(route_pe, 1)
            dve.wait_ge(late_w_in, 16 * 5)
            then(vec.scalar_tensor_tensor(rt[:, 0, :], b_s[0:GRAPHS, 0:E], 1.0 / NODES,
                                          br_bc[:, :], ALU.mult, ALU.add))
            then(vec.tensor_reduce(columns(0), rt[:, 0, :], AX.X, ALU.max, negate=True))
            dve.wait_ge(route_act, 1)
            then(vec.reciprocal(columns(2), columns(1)))
            then(vec.tensor_scalar(rt[:, 2, :], rt[:, 1, :], columns(2), None, ALU.mult))
            dve.wait_ge(route_pe, 2)
            then(vec.tensor_scalar(rt[:, 3, :], b_s[0:GRAPHS, E:2 * E], float(NODES), None, ALU.mult))
            then(vec.reciprocal(rt[:, 6, :], rt[:, 3, :]))
            then(vec.tensor_scalar(rt[:, 7, :], rt[:, 6, :], CAPACITY, 1.0, ALU.mult, ALU.min))
            then(vec.tensor_tensor(rt[:, 4, :], rt[:, 2, :], rt[:, 7, :], ALU.mult))
            then(vec.tensor_reduce(columns(3), rt[:, 4, :], AX.X, ALU.max, negate=True))
            dve.wait_ge(route_act, 2)
            then(vec.reciprocal(columns(5), columns(4)))
            then(vec.tensor_scalar(rt[:, 8, :], rt[:, 5, :], columns(5), None, ALU.mult))
            then(vec.max(rt[:, 9, :], rt[:, 8, :]))
            then(vec.max_index(top_at[:, :], rt[:, 9, :], rt[:, 8, :]))
            then(vec.tensor_tensor(columns(6), rt[:, 9, 1:2], rt[:, 9, 0:1], ALU.subtract))
            then(vec.tensor_copy(picked[:, TOP:2 * TOP], top_at[:, 0:TOP]))
            dve.wait_ge(route_act, 3)
            then(vec.tensor_scalar(columns(8), columns(7), 1.0, None, ALU.add))
            then(vec.reciprocal(picked[:, 0:1], columns(8)))
            then(vec.tensor_tensor(picked[:, 1:2], picked[:, 0:1], columns(7), ALU.mult))
            dve.wait_ge(const_ready, 2)
            dve.wait_ge(ident_ready, 1)
            then(vec.tensor_tensor(picked_diag[:, :, :], repeat(ident[0:GRAPHS, 0:GRAPHS], 2 * TOP),
                                   picked[:, :].unsqueeze(2).broadcast_to([GRAPHS, 2 * TOP, GRAPHS]),
                                   ALU.mult))
            for k in range(TOP):
                then(vec.tensor_scalar(rt[:, 10 + k, :], iota_e[:, :], picked[:, TOP + k:TOP + k + 1],
                                       picked[:, k:k + 1], ALU.is_equal, ALU.mult))
            then(vec.tensor_tensor(rt[:, 12, :], rt[:, 10, :], rt[:, 11, :], ALU.add))
            dve.wait_ge(route_pe, 3)
            vec.tensor_copy(expert[:, :, :], b_t[0:1, TOP * GRAPHS:2 * TOP * GRAPHS]
                            .rearrange("p (k b) -> p b k", k=TOP)).then_inc(experts_ready, 1)
            vec.tensor_copy(w_bc[:, :, :], b_t[:, 0:TOP * GRAPHS]
                            .rearrange("p (k b) -> p k b", k=TOP)).then_inc(experts_ready, 1)
            dve.wait_ge(route_pe, 4)
            vec.tensor_copy(denseT[:, :], b_s[0:E, 0:GRAPHS]).then_inc(route_dve, 1)
            dve.wait_ge(route_pe, 5)
            vec.tensor_copy(bias2[:, :], b_y[0:GRAPHS, 0:D]).then_inc(bias2_ready, 1)
            dve.wait_ge(experts_ready, 2)

            def z_of(g, j, k):
                b = g * G + j
                by = y_banks[j]
                at = k * D
                if k == 0:
                    dve.wait_ge(e_in_psum, b + 1)
                    if j == 0:
                        dve.wait_ge(res_ready, g + 1)
                else:
                    dve.wait_ge(z0_done, b + 1)
                vec.scalar_tensor_tensor(graph(xl_res, b), by[:, at:at + D],
                                         w_bc[:, k, bass.ds(b, 1)], graph(xl_res, b),
                                         ALU.mult, ALU.add).then_inc((z0_done, z_done)[k], 1)

            def z_stats(b, j):
                vec.bn_stats(stats[:, 0, j, :], graph(xl_res, b)).then_inc(zstats_done, 1)

            def aggregate(g):
                for j in range(G):
                    op = vec.bn_aggr(mv[:, 0, j, :], stats[:, 0, j, :])
                op.then_inc(ln2_chain, 1)

            def chain_op(g, n):
                base = (CHAIN + 1) * g
                if n < 0:
                    dve.wait_ge(ln2_chain, base + 1)
                    vec.tensor_scalar(var_eps[:, 0:G], mv[:, 0, 0:G, 1], LN_EPS, None,
                                      ALU.add).then_inc(ln2_chain, 1)
                elif n < RSQRT_OPS:
                    if n == RSQRT_OPS - 1:
                        wait(dve, unit_ready, g)
                    rsqrt_op(n, ln2_chain, base + 1, 0, G, rstd[:, 0, 0:G], ln2_chain)
                else:
                    dve.wait_ge(ln2_chain, base + RSQRT_OPS + 2)
                    vec.scalar_tensor_tensor(neg_mr[:, :], mv[:, 0, 0:G, 0], -1.0, rstd[:, 0, 0:G],
                                             ALU.mult, ALU.mult).then_inc(ln2_ready, 1)

            def final(g, part):
                u, x1 = by_graph(group(xl_res, g)), by_graph(group(x_res, g))
                if part == 0:
                    dve.wait_ge(unit_ready, g + 1)
                    vec.tensor_tensor(u, u, repeat(gamma_bc[:, :], G), ALU.mult).then_inc(scaled, 1)
                elif part == 1:
                    vec.tensor_tensor(x1, x1, repeat(beta_bc[:, :], G), ALU.add).then_inc(shifted, 1)
                else:
                    dve.wait_ge(scaled, g + 1)
                    dve.wait_ge(shifted, g + 1)
                    vec.tensor_tensor(x1, x1, u, ALU.add).then_inc(final_ready, 1)

            def group_step(g, zs, chain, finals):
                if chain:
                    dve.wait_ge(zstats_done, g * G)
                n = -1
                for j in range(G):
                    if zs:
                        z_of(g, j, 0)
                    if chain and j == 0:
                        aggregate(g - 1)
                    if zs and j > 0:
                        dve.wait_ge(z_done, g * G + j)
                    if chain:
                        chain_op(g - 1, n)
                    if zs and j > 0:
                        z_stats(g * G + j - 1, j - 1)
                    if chain:
                        chain_op(g - 1, n + 1)
                    if zs:
                        z_of(g, j, 1)
                    if chain and n + 2 < RSQRT_OPS + 1:
                        chain_op(g - 1, n + 2)
                    n += 3
                    if finals and j in (1, 2):
                        final(g - 2, j - 1)
                if chain:
                    for n in range(n, RSQRT_OPS + 1):
                        chain_op(g - 1, n)
                if zs:
                    dve.wait_ge(z_done, g * G + G)
                if finals:
                    final(g - 2, 2)
                if zs:
                    z_stats(g * G + G - 1, G - 1)

            group_step(0, True, False, False)
            group_step(1, True, True, False)
            with dve.Fori(2, GROUPS) as g:
                group_step(g, True, True, True)
            group_step(GROUPS, False, True, True)
            group_step(GROUPS + 1, False, False, True)

        @block.tensor
        def _(pe):
            pe.wait_ge(ident_ready, 1)
            pe.wait_ge(rows_in, 16 * 4)
            nc.tensor.transpose(b_t[:, 0:NROWS], bias_rows[:, :],
                                ident[0:NROWS, 0:NROWS]).then_inc(cols_in_psum, 1)
            pe.wait_ge(cols_ready, 2)
            pe.wait_ge(gnn_w_in, 16 * 5)

            def transposes(dst, src, done):
                for j in range(G):
                    op = nc.tensor.transpose(dst[:, j * P:(j + 1) * P], src[:, j * P:(j + 1) * P],
                                             ident[:, :])
                op.then_inc(done, 1)

            def products(dst, left, right, done):
                for j in range(G):
                    cut = slice(j * P, (j + 1) * P)
                    op = nc.tensor.matmul(dst[:, cut], left[:, cut],
                                          right[:, cut] if right.shape[-1] == GD else right,
                                          start=True, stop=True)
                op.then_inc(done, 1)

            def step(i, c):
                s = 2 * i + c
                g = s - 2
                if live(g):
                    pe.wait_ge(prob_ready, g + 1)
                    wait(pe, xlT_ready, g - 1)
                    transposes(b_p, prob, probT_in_psum)
                g = s
                if live(g):
                    pe.wait_ge(xn_ready, g + 1)
                    wait(pe, xnT_ready, g)
                    transposes(b_t, xn[:, c % 2, :], xnT_in_psum)
                g = s - 1
                if live(g):
                    pe.wait_ge(q_ready, g + 1)
                    pe.wait_ge(k_ready, g + 1)
                    wait(pe, scores_masked, g)
                    products(b_s, qT, kT, scores_in_psum)
                    pe.wait_ge(v_ready, g + 1)
                    wait(pe, vw_ready, g)
                    products(b_w, vT, wo_sb[:, :], vw_in_psum)
                g = s - 2
                if live(g):
                    pe.wait_ge(probT_ready, g + 1)
                    pe.wait_ge(vw_ready, g + 1)
                    wait(pe, rel_ready, g)
                    products(b_y, probT, vw[:, c % 2, :], y_in_psum)
                g = s
                if live(g):
                    pe.wait_ge(xnT_ready, g + 1)
                    for w, dst, done, free in ((wq_sb, b_q, q_in_psum, q_ready),
                                               (wk_sb, b_k, k_in_psum, k_ready),
                                               (wv_sb, b_v, v_in_psum, v_ready)):
                        wait(pe, free, g)
                        nc.tensor.matmul(dst[:, :], w[:, :], xnT[:, :], start=True,
                                         stop=True).then_inc(done, 1)
                g = s - 3
                if live(g):
                    pe.wait_ge(xl_ready, g + 1)
                    if live(s - 2):
                        wait(pe, probT_ready, s - 1)
                    else:
                        wait(pe, xlT_ready, g)
                    transposes(b_p, xl[:, (c + 1) % 2, :], xlT_in_psum)

            run_steps(pe, step, 0, 4, 16, GROUPS + 3)

            pe.wait_ge(mean_done, GROUPS)
            pe.wait_ge(late_w_in, 16 * 5)
            pe.wait_ge(const_ready, 2)
            nc.tensor.matmul(b_s[0:GRAPHS, 0:E], mean_sum[:, :], wr_sb[:, :], start=True,
                             stop=True).then_inc(route_pe, 1)
            pe.wait_ge(route_dve, 4)
            nc.tensor.matmul(b_s[0:GRAPHS, E:2 * E], ones[0:GRAPHS, 0:GRAPHS], rt[:, 2, :],
                             start=True, stop=True).then_inc(route_pe, 1)
            pe.wait_ge(route_dve, 19)
            nc.tensor.matmul(b_t[:, 0:2 * TOP * GRAPHS], ones[0:GRAPHS, 0:P],
                             picked_diag[:, :, :].rearrange("b q c -> b (q c)"), start=True,
                             stop=True).then_inc(route_pe, 1)
            pe.wait_ge(route_dve, 22)
            nc.tensor.transpose(b_s[0:E, 0:GRAPHS], rt[:, 12, :],
                                ident[0:GRAPHS, 0:GRAPHS]).then_inc(route_pe, 1)
            pe.wait_ge(route_dve, 23)
            nc.tensor.matmul(b_y[0:GRAPHS, 0:D], denseT[:, :], b2_sb[:, :], start=True,
                             stop=True).then_inc(route_pe, 1)

            pe.wait_ge(w2_in, 16)
            pe.wait_ge(experts_ready, 2)
            pe.wait_ge(xlT_ready, GROUPS)

            def hidden(g, j):
                b = g * G + j
                pe.wait_ge(w1_picked, b + 1)
                wait(pe, gelu_done, b - 1)
                for k in range(TOP):
                    for f in range(FC):
                        at = (k * FC + f) * P
                        op = nc.tensor.matmul((b_q, b_k)[j % 2][:, at:at + P],
                                              w1_pick[:, j % 2, k, f * P:(f + 1) * P],
                                              graph(xlT_res, b), start=True, stop=True)
                op.then_inc(h_in_psum, 1)

            def experts(b, j):
                pe.wait_ge(gelu_done, b + 1)
                wait(pe, z_done, b - G + 1)
                for k in range(TOP):
                    e = pe.value_load(expert[0:1, bass.ds(b, 1), k], min_val=0, max_val=E - 1)
                    at = k * D
                    for f in range(FC):
                        op = nc.tensor.matmul(y_banks[j][:, at:at + D],
                                              hT[:, j % 2, (k * FC + f) * P:(k * FC + f + 1) * P],
                                              w2_sb[:, bass.ds(e * (FC * D) + f * D, D)],
                                              start=(f == 0), stop=(f == FC - 1))
                op.then_inc(e_in_psum, 1)

            def group_step(g, first):
                hidden(g, 0)
                if not first:
                    experts(g * G - 1, G - 1)
                for j in range(1, G):
                    hidden(g, j)
                    experts(g * G + j - 1, j - 1)

            group_step(0, True)
            with pe.Fori(1, GROUPS) as g:
                group_step(g, False)
            experts(GRAPHS - 1, G - 1)


_INS = ["x", "adj", "L0_gnn_Wv", "L0_gnn_bv", "L0_gnn_Wk", "L0_gnn_bk", "L0_gnn_Wq", "L0_gnn_bq",
        "L0_gnn_Wo", "L0_gnn_bo", "L0_ffn_Wr", "L0_ffn_br", "L0_ffn_W1", "L0_ffn_b1", "L0_ffn_W2",
        "L0_ffn_b2", "L0_ffn_gamma", "L0_ffn_beta"]


def kernel(**inputs):
    import numpy as np
    import concourse.bacc as bacc
    from concourse.bass_utils import run_bass_kernel_spmd

    nc = bacc.Bacc("TRN2", target_bir_lowering=False, num_devices=1)
    arrays, args = {}, []
    for name in _INS:
        a = np.ascontiguousarray(inputs[name])
        arrays["in_" + name] = a
        args.append(nc.dram_tensor("in_" + name, a.shape, mybir.dt.from_np(a.dtype),
                                   kind="ExternalInput").ap())
    result = nc.dram_tensor("out_0", inputs["x"].shape, F32, kind="ExternalOutput").ap()
    build(nc, *args, result)
    r = run_bass_kernel_spmd(nc, [arrays], core_ids=[0])
    return r.results[0]["out_0"]
```

```python
from contextlib import ExitStack

import concourse.bass as bass
from concourse import mybir

F32 = mybir.dt.float32
I32 = mybir.dt.int32
U32 = mybir.dt.uint32
ALU = mybir.AluOpType
ACT = mybir.ActivationFunctionType
AX = mybir.AxisListType

P = 128
G = 4
TOP = 2
NEG = 9000000000000000.0
LN_EPS = 1e-5
RSQRT_MAGIC = float(0x5F3759DF)
NEWTONS = 3
CHAIN1 = 4
CHAIN2 = 4 + 3 * NEWTONS
CAPACITY_FACTOR = 1.25


def wait(engine, semaphore, value):
    if not isinstance(value, int) or value > 0:
        engine.wait_ge(semaphore, value)


def after(engine, semaphore, i):
    if not isinstance(i, int):
        engine.wait_ge(semaphore, 1)


def run_steps(engine, body, first, loop_from, loop_to, end):
    for s in range(first, loop_from):
        body(0, s)
    with engine.Fori(loop_from // 2, loop_to // 2) as i:
        body(i, 0)
        body(i, 1)
    for s in range(loop_to, end):
        body(0, s)


def build(nc, x, adj, Wv, bv, Wk, bk, Wq, bq, Wo, bo, Wr, br, W1, b1, W2, b2, gamma, beta, out):
    GRAPHS, NODES, D = x.shape
    E, _, FF = W1.shape
    FC = FF // P
    GROUPS = GRAPHS // G
    GD = G * D
    W1C = FF + FC
    CAPACITY = float(-(-GRAPHS * NODES * CAPACITY_FACTOR // E))
    assert NODES == P and D == P and FF % P == 0 and GRAPHS % (2 * G) == 0

    def live(g):
        return not isinstance(g, int) or 0 <= g < GROUPS

    def chained(s):
        return live(s + 2) or live(s - 3)

    def ln_columns(s):
        return 0 if live(s + 2) else G, 2 * G if live(s - 3) else G

    bias2_dram = nc.dram_tensor("bias2_scratch", (GRAPHS, D), F32).ap()

    ctx = ExitStack()
    with ctx:
        def sb(name, shape, dt=F32):
            return ctx.enter_context(nc.sbuf_tensor(name, shape, dt))

        def bank(name):
            return ctx.enter_context(nc.psum_tensor(name, [P, GD], F32))

        def sem(name):
            return ctx.enter_context(nc.semaphore(name))

        x_res = sb("x_res", [P, GRAPHS * D])
        xl_res = sb("xl_res", [P, GRAPHS * D])
        xlT_res = sb("xlT_res", [P, GRAPHS * P])
        b2bc = sb("b2bc", [P, GRAPHS * D])
        w1_sb = sb("w1_sb", [P, E * W1C])
        w1v = w1_sb[:, :].rearrange("p (e c) -> p e c", e=E)
        w2_sb = sb("w2_sb", [P, E * FC * D])
        wq_sb, wk_sb, wv_sb, wo_sb = (sb(n, [P, D]) for n in ("wq_sb", "wk_sb", "wv_sb", "wo_sb"))
        wr_sb = sb("wr_sb", [P, E])
        bo_bc = sb("bo_bc", [P, D])
        gamma_bc = sb("gamma_bc", [P, D])
        beta_bc = sb("beta_bc", [P, D])
        br_bc = sb("br_bc", [GRAPHS, E])
        b2_sb = sb("b2_sb", [E, D])
        NROWS = 3 + E * FC
        bias_rows = sb("bias_rows", [NROWS, P])
        bias_cols = sb("bias_cols", [P, 3])
        ident = sb("ident", [P, P])
        ones = sb("ones", [P, W1C])

        adj_sb = sb("adj_sb", [P, 2, GD])
        xn = sb("xn", [P, 2, GD])
        xnT = sb("xnT", [P, GD])
        qT = sb("qT", [P, GD])
        kT = sb("kT", [P, GD])
        vT = sb("vT", [P, GD])
        vw = sb("vw", [P, 2, GD])
        neg_mask = sb("neg_mask", [P, GD])
        score = sb("score", [P, GD])
        prob = sb("prob", [P, GD])
        probT = sb("probT", [P, GD])
        rel = sb("rel", [P, GD])
        xl = sb("xl", [P, 2, GD])
        neg_max = sb("neg_max", [P, 2, G])
        den = sb("den", [P, 2, G])
        rden = sb("rden", [P, 2, G])
        mean_sum = sb("mean_sum", [P, GRAPHS])
        stats = sb("stats", [P, 2, 2 * G, 6])
        mv = sb("mv", [P, 2, 2 * G, 2])
        neg_mean = sb("neg_mean", [P, 2, 2 * G])
        rstd = sb("rstd", [P, 2, 2 * G])
        var_eps = sb("var_eps", [P, 2 * G])
        halved = sb("halved", [P, 2 * G], I32)
        guess = sb("guess", [P, 2 * G], I32)
        log_var = sb("log_var", [P, 2 * G])
        rough = sb("rough", [P, 2 * G])
        newton_y = sb("newton_y", [P, 2 * G])
        newton_t = sb("newton_t", [P, 2 * G])

        rt = sb("rt", [GRAPHS, 16, E])
        r1 = sb("r1", [GRAPHS, 16])
        top_at = sb("top_at", [GRAPHS, E], U32)
        picked = sb("picked", [GRAPHS, 2 * TOP])
        picked_diag = sb("picked_diag", [GRAPHS, 2 * TOP, GRAPHS])
        w_bc = sb("w_bc", [P, TOP, GRAPHS])
        w1_at = sb("w1_at", [1, GRAPHS * TOP], I32)
        w2_at = sb("w2_at", [1, GRAPHS * TOP], I32)
        iota_e = sb("iota_e", [GRAPHS, E])
        denseT = sb("denseT", [E, GRAPHS])
        bias2 = sb("bias2", [GRAPHS, D])

        w1_pick = sb("w1_pick", [P, G, TOP, W1C])
        hT = sb("hT", [P, G, TOP * FC * P])
        neg_mr = sb("neg_mr", [P, G])

        b_p, b_t, b_s, b_y, b_q, b_k, b_v, b_w = (bank("bank_" + n) for n in "ptsyqkvw")
        h_banks, y_banks = (b_q, b_k, b_p, b_y), (b_v, b_w, b_s, b_t)

        x_in = [sem(f"x_in{n}") for n in range(2)]
        adj_in = [sem(f"adj_in{n}") for n in range(2)]
        gnn_w_in, rows_in, late_w_in, w1_in, w2_in = (
            sem(n) for n in ("gnn_w_in", "rows_in", "late_w_in", "w1_in", "w2_in"))
        zeroed, ident_ready, const_ready = sem("zeroed"), sem("ident_ready"), sem("const_ready")
        cols_in_psum, cols_ready = sem("cols_in_psum"), sem("cols_ready")
        stats1_done, stats2_done = sem("stats1_done"), sem("stats2_done")
        centred = [sem("xn_centred"), sem("xl_centred")]
        ln_chain, log_ready, guess_ready, ln_ready = (
            sem("ln_chain"), sem("log_ready"), sem("guess_ready"), sem("ln_ready"))
        xn_ready, xnT_in_psum, xnT_ready = sem("xn_ready"), sem("xnT_in_psum"), sem("xnT_ready")
        q_in_psum, k_in_psum, v_in_psum = sem("q_in_psum"), sem("k_in_psum"), sem("v_in_psum")
        q_ready, k_ready, v_ready = sem("q_ready"), sem("k_ready"), sem("v_ready")
        vw_in_psum, vw_ready = sem("vw_in_psum"), sem("vw_ready")
        scores_in_psum, scores_masked = sem("scores_in_psum"), sem("scores_masked")
        neg_mask_ready, score_ready, max_ready = (
            sem("neg_mask_ready"), sem("score_ready"), sem("max_ready"))
        prob_ready, probT_in_psum, probT_ready = (
            sem("prob_ready"), sem("probT_in_psum"), sem("probT_ready"))
        rden_ready, y_in_psum, rel_ready, x1_ready = (
            sem("rden_ready"), sem("y_in_psum"), sem("rel_ready"), sem("x1_ready"))
        xl_ready, xlT_in_psum, xlT_ready, mean_done = (
            sem("xl_ready"), sem("xlT_in_psum"), sem("xlT_ready"), sem("mean_done"))
        xl_saved = [sem(f"xl_saved{n}") for n in range(2)]
        route_pe, route_dve, route_act = sem("route_pe"), sem("route_dve"), sem("route_act")
        experts_ready = sem("experts_ready")
        bias2_ready, bias2_out, bias2_in = sem("bias2_ready"), sem("bias2_out"), sem("bias2_in")
        w1_picked, h_in_psum, gelu_done, e_in_psum = (
            sem("w1_picked"), sem("h_in_psum"), sem("gelu_done"), sem("e_in_psum"))
        res_ready = sem("group_res_ready")
        z0_done, z_done, zstats_done = sem("z0_done"), sem("z_done"), sem("zstats_done")
        ln2_chain, ln2_ready, unit_ready = (
            sem("ln2_chain"), sem("group_ln2_ready"), sem("group_unit_ready"))
        scaled, shifted, final_ready, out_done = (
            sem("group_scaled"), sem("group_shifted"), sem("group_final_ready"), sem("out_done"))

        def group(tensor, g):
            return tensor[:, bass.ds(g * GD, GD)]

        def graph(tensor, b):
            return tensor[:, bass.ds(b * D, D)]

        def places(engine, table, first, graphs, stride):
            at = table[0:1, bass.ds(first * TOP, graphs * TOP)]
            _, values = nc.values_load_multi_w_load_instructions(
                at, engines=[engine], min_val=0, max_val=(E - 1) * stride,
                skip_runtime_bounds_check_because="top-2 of E experts")
            return values

        def by_graph(ap):
            return ap.rearrange("p (g n) -> p g n", g=G)

        def repeat(ap, times):
            return ap.unsqueeze(1).broadcast_to([ap.shape[0], times, ap.shape[1]])

        block = ctx.enter_context(nc.Block())

        @block.sync
        def _(sp):
            x_v = x.rearrange("b n d -> n b d")
            adj_v = adj.rearrange("b n m -> n b m")

            def load_x(i):
                for n in range(2):
                    wait(sp, x_in[n], 16 * i)
                    after(sp, x_in[n], i)
                    sp.dma_start(by_graph(group(x_res, 2 * i + n)),
                                 x_v[:, bass.ds((2 * i + n) * G, G), :]).then_inc(x_in[n], 16)

            def load_adj(i):
                for n in range(2):
                    g = 2 * i + n
                    wait(sp, adj_in[n], 16 * i)
                    wait(sp, neg_mask_ready, g - 1)
                    wait(sp, scores_masked, g - 1)
                    after(sp, adj_in[n], i)
                    sp.dma_start(by_graph(adj_sb[:, n, :]),
                                 adj_v[:, bass.ds(g * G, G), :]).then_inc(adj_in[n], 16)

            load_x(0)
            load_adj(0)
            load_x(1)
            load_x(2)
            load_adj(1)
            with sp.Fori(2, GROUPS // 2 - 1) as i:
                load_x(i + 1)
                load_adj(i)
            load_adj(GROUPS // 2 - 1)
            sp.dma_start(w1v[:, :, 0:FF], W1.rearrange("e d f -> d e f")).then_inc(w1_in, 16)
            sp.dma_start(w2_sb[:, :].rearrange("p (e c d) -> p e c d", e=E, c=FC),
                         W2.rearrange("e (c p) d -> p e c d", p=P)).then_inc(w2_in, 16)
            sp.wait_ge(bias2_ready, 1)
            sp.dma_start(bias2_dram, bias2[:, :]).then_inc(bias2_out, 16)
            sp.wait_ge(bias2_out, 16)
            sp.dma_start(b2bc[:, 0:GD], bias2_dram[0:G, :].rearrange("b d -> (b d)").unsqueeze(0)
                         .broadcast_to([P, GD])).then_inc(bias2_in, 16)
            sp.wait_ge(bias2_in, 16)
            sp.dma_start(b2bc[:, GD:], bias2_dram[G:, :].rearrange("b d -> (b d)").unsqueeze(0)
                         .broadcast_to([P, (GROUPS - 1) * GD])).then_inc(bias2_in, 16)
            out_v = out.rearrange("b n d -> n b d")

            def store(g):
                sp.wait_ge(final_ready, g + 1)
                after(sp, final_ready, g)
                sp.dma_start(out_v[:, bass.ds(g * G, G), :],
                             by_graph(group(x_res, g))).then_inc(out_done, 16)

            with sp.Fori(0, GROUPS) as g:
                store(g)
            sp.wait_ge(out_done, 16 * GROUPS)

        @block.gpsimd
        def _(pool):
            nc.gpsimd.memset(ident[:, :], 0.0).then_inc(zeroed, 1)
            nc.gpsimd.memset(ones[:, :], 1.0).then_inc(const_ready, 1)
            nc.gpsimd.iota(iota_e[:, :], pattern=[[1, E]], base=0, channel_multiplier=0,
                           allow_small_or_imprecise_dtypes=True).then_inc(const_ready, 1)
            pool.wait_ge(zeroed, 1)
            nc.gpsimd.affine_select(out=ident[:, :], in_=ident[:, :], compare_op=ALU.not_equal,
                                    fill=1.0, base=0, pattern=[[-1, P]],
                                    channel_multiplier=1).then_inc(ident_ready, 1)

            def normalise(dst, g, par, ln, ready):
                def each(ap):
                    return ap[:, par, ln * G:(ln + 1) * G].unsqueeze(2).broadcast_to([P, G, D])

                nc.gpsimd.tensor_tensor(by_graph(dst), by_graph(group(x_res, g)), each(neg_mean),
                                        ALU.add).then_inc(centred[ln], 1)
                wait(pool, centred[ln], g + 1)
                nc.gpsimd.tensor_tensor(by_graph(dst), by_graph(dst), each(rstd),
                                        ALU.mult).then_inc(ready, 1)

            def step(i, c):
                s = 2 * i + c
                g = s + 1
                if live(g):
                    wait(pool, ln_ready, g + 1)
                    wait(pool, xnT_in_psum, g - 1)
                    normalise(xn[:, (c + 1) % 2, :], g, (c + 1) % 2, 0, xn_ready)
                g = s - 1
                if live(g):
                    wait(pool, scores_masked, g + 1)
                    wait(pool, neg_mask_ready, g + 1)
                    nc.gpsimd.tensor_tensor(score[:, :], score[:, :], neg_mask[:, :],
                                            ALU.add).then_inc(score_ready, 1)
                if live(s):
                    pool.wait_ge(adj_in[c % 2], 16 * (i + c // 2 + 1))
                    wait(pool, score_ready, s)
                g = s - 3
                if live(g):
                    wait(pool, ln_ready, g + 6)
                    wait(pool, xlT_in_psum, g - 1)
                    wait(pool, xl_saved[(c + 1) % 2], 16 * (i + (c - 3) // 2))
                    normalise(xl[:, (c + 1) % 2, :], g, c % 2, 1, xl_ready)
                g = s
                if live(g):
                    nc.gpsimd.tensor_scalar(neg_mask[:, :], adj_sb[:, c % 2, :], -1.0, NEG,
                                            ALU.add, ALU.mult).then_inc(neg_mask_ready, 1)

            run_steps(pool, step, -1, 6, 14, GROUPS + 3)

            pool.wait_ge(experts_ready, 1)
            pool.wait_ge(w1_in, 16)
            pool.wait_ge(cols_ready, 2)

            def pick(g, j, at):
                b = g * G + j
                wait(pool, gelu_done, b - G + 1)
                for k in range(TOP):
                    last = nc.gpsimd.tensor_tensor(w1_pick[:, j, k, :],
                                                   w1_sb[:, bass.ds(at[j * TOP + k], W1C)],
                                                   ones[:, :], ALU.mult)
                last.then_inc(w1_picked, 1)

            def residual(g, b2_count):
                pool.wait_ge(bias2_in, b2_count)
                nc.gpsimd.tensor_tensor(group(xl_res, g), group(xl_res, g), group(b2bc, g),
                                        ALU.add).then_inc(res_ready, 1)

            at = places(mybir.EngineType.Pool, w1_at, 0, G, W1C)
            pick(0, 0, at)
            pick(0, 1, at)
            for n in range(2):
                pool.wait_ge(xl_saved[n], 16 * (GROUPS // 2))
            residual(0, 16)
            pick(0, 2, at)
            pick(0, 3, at)
            with pool.Fori(1, GROUPS) as g:
                at = places(mybir.EngineType.Pool, w1_at, g * G, G, W1C)
                pick(g, 0, at)
                pick(g, 1, at)
                residual(g, 32)
                pick(g, 2, at)
                pick(g, 3, at)

        @block.scalar
        def _(act):
            nc.scalar.preload_act_table_set("natural_log_exp_and_others")
            for n, src in enumerate((bq, bk, bv)):
                act.dma_start(bias_rows[n:n + 1, :], src.unsqueeze(0)).then_inc(rows_in, 16)
            act.dma_start(bias_rows[3:NROWS, :],
                          b1.rearrange("e (c p) -> (e c) p", p=P)).then_inc(rows_in, 16)
            for dst, src in ((wq_sb, Wq), (wk_sb, Wk), (wv_sb, Wv), (wo_sb, Wo)):
                act.dma_start(dst[:, :], src).then_inc(gnn_w_in, 16)
            act.dma_start(bo_bc[:, :], bo.unsqueeze(0).broadcast_to([P, D])).then_inc(gnn_w_in, 16)
            act.dma_start(wr_sb[:, :], Wr).then_inc(late_w_in, 16)
            act.dma_start(br_bc[:, :], br.unsqueeze(0).broadcast_to([GRAPHS, E])).then_inc(late_w_in, 16)
            act.dma_start(b2_sb[:, :], b2).then_inc(late_w_in, 16)
            for dst, src in ((gamma_bc, gamma), (beta_bc, beta)):
                act.dma_start(dst[:, :], src.unsqueeze(0).broadcast_to([P, D])).then_inc(late_w_in, 16)
            act.wait_ge(cols_ready, 1)

            def relu_of(dst, src, n, ready):
                nc.scalar.activation(dst[:, :], src[:, :], ACT.Relu,
                                     bias=bias_cols[:, n:n + 1]).then_inc(ready, 1)

            def step(i, c):
                s = 2 * i + c
                g = s
                if live(g):
                    act.wait_ge(xnT_in_psum, g + 1)
                    wait(act, v_in_psum, g)
                    nc.scalar.activation(xnT[:, :], b_t[:, :], ACT.Copy).then_inc(xnT_ready, 1)
                g = s - 2
                if live(g):
                    act.wait_ge(probT_in_psum, g + 1)
                    wait(act, y_in_psum, g)
                    nc.scalar.activation(probT[:, :], b_p[:, :], ACT.Copy).then_inc(probT_ready, 1)
                if chained(s):
                    lo, hi = ln_columns(s)
                    act.wait_ge(ln_chain, CHAIN1 * (s + 2) + 2)
                    wait(act, ln_ready, s + 2)
                    nc.scalar.activation(log_var[:, lo:hi], var_eps[:, lo:hi],
                                         ACT.Ln).then_inc(log_ready, 1)
                    act.wait_ge(log_ready, s + 3)
                    nc.scalar.activation(rough[:, lo:hi], log_var[:, lo:hi], ACT.Exp,
                                         scale=-0.5).then_inc(guess_ready, 1)
                g = s - 4
                if live(g):
                    act.wait_ge(xlT_in_psum, g + 1)
                    nc.scalar.activation(group(xlT_res, g), b_t[:, :],
                                         ACT.Copy).then_inc(xlT_ready, 1)
                    act.wait_ge(xl_ready, g + 1)
                    act.dma_start(group(xl_res, g),
                                  xl[:, c % 2, :]).then_inc(xl_saved[c % 2], 16)
                g = s
                if live(g):
                    act.wait_ge(q_in_psum, g + 1)
                    wait(act, scores_in_psum, g)
                    relu_of(qT, b_q, 0, q_ready)
                g = s - 2
                if live(g):
                    act.wait_ge(y_in_psum, g + 1)
                    act.wait_ge(rden_ready, g + 1)
                    wait(act, x1_ready, g)
                    for j in range(G):
                        last = nc.scalar.activation(rel[:, j * D:(j + 1) * D],
                                                    b_y[:, j * D:(j + 1) * D], ACT.Relu,
                                                    scale=rden[:, c % 2, j:j + 1])
                    last.then_inc(rel_ready, 1)
                g = s
                if live(g):
                    act.wait_ge(k_in_psum, g + 1)
                    relu_of(kT, b_k, 1, k_ready)
                    act.wait_ge(v_in_psum, g + 1)
                    wait(act, vw_in_psum, g)
                    relu_of(vT, b_v, 2, v_ready)
                g = s - 1
                if live(g):
                    act.wait_ge(max_ready, g + 1)
                    wait(act, probT_in_psum, g)
                    wait(act, rden_ready, g - 1)
                    for j in range(G):
                        last = nc.scalar.activation(
                            prob[:, j * P:(j + 1) * P], score[:, j * P:(j + 1) * P], ACT.Exp,
                            bias=neg_max[:, (c + 1) % 2, j:j + 1],
                            accum_out=den[:, (c + 1) % 2, j:j + 1])
                    last.then_inc(prob_ready, 1)

            run_steps(act, step, -2, 6, 12, GROUPS + 4)

            act.wait_ge(route_dve, 2)
            nc.scalar.activation(rt[:, 1, :], rt[:, 0, :], ACT.Exp, bias=r1[:, 0:1],
                                 accum_out=r1[:, 1:2]).then_inc(route_act, 1)
            act.wait_ge(route_dve, 9)
            nc.scalar.activation(rt[:, 5, :], rt[:, 4, :], ACT.Exp, bias=r1[:, 3:4],
                                 accum_out=r1[:, 4:5]).then_inc(route_act, 1)
            act.wait_ge(route_dve, 14)
            nc.scalar.activation(r1[:, 7:8], r1[:, 6:7], ACT.Exp).then_inc(route_act, 1)

            nc.scalar.preload_act_table(ACT.Gelu)

            def gelu(g, j):
                b = g * G + j
                act.wait_ge(h_in_psum, b + 1)
                wait(act, e_in_psum, b - G + 1)
                for k in range(TOP):
                    for f in range(FC):
                        at = (k * FC + f) * P
                        last = nc.scalar.activation(
                            hT[:, j, at:at + P], h_banks[j][:, at:at + P], ACT.Gelu,
                            bias=w1_pick[:, j, k, FF + f:FF + f + 1])
                last.then_inc(gelu_done, 1)

            def unit(g, j):
                if j == 0:
                    wait(act, ln2_ready, g + 1)
                last = nc.scalar.activation(graph(xl_res, g * G + j), graph(xl_res, g * G + j),
                                            ACT.Identity, scale=rstd[:, 0, j:j + 1],
                                            bias=neg_mr[:, j:j + 1])
                if j == G - 1:
                    last.then_inc(unit_ready, 1)

            def group_step(g, gelus, units):
                for j in range(G):
                    if gelus:
                        gelu(g, j)
                    if units and j >= 2:
                        unit(g - 2, 2 * j - 4)
                        unit(g - 2, 2 * j - 3)

            group_step(0, True, False)
            group_step(1, True, False)
            with act.Fori(2, GROUPS) as g:
                group_step(g, True, True)
            group_step(GROUPS, False, True)
            group_step(GROUPS + 1, False, True)

        @block.vector
        def _(dve):
            def rsqrt_op(n, chain, base, lo, hi, dst, ready):
                v, t, y = var_eps[:, lo:hi], newton_t[:, lo:hi], newton_y[:, lo:hi]
                dve.wait_ge(chain, base + n + 1)
                if n == 0:
                    op = nc.vector.tensor_scalar(halved[:, lo:hi], v.bitcast(I32), 1, None,
                                                 ALU.logical_shift_right)
                elif n == 1:
                    op = nc.vector.tensor_scalar(guess[:, lo:hi], halved[:, lo:hi], -1.0,
                                                 RSQRT_MAGIC, ALU.mult, ALU.add)
                else:
                    r, m = divmod(n - 2, 3)
                    prev = guess[:, lo:hi].bitcast(F32) if r == 0 else y
                    if m == 0:
                        op = nc.vector.tensor_tensor(t, prev, prev, ALU.mult)
                    elif m == 1:
                        op = nc.vector.scalar_tensor_tensor(t, t, -0.5, v, ALU.mult, ALU.mult)
                    else:
                        to = dst if r == NEWTONS - 1 else y
                        op = nc.vector.scalar_tensor_tensor(to, t, 1.5, prev, ALU.add, ALU.mult)
                op.then_inc(ready if n == 1 + 3 * NEWTONS else chain, 1)

            RSQRT_OPS = 2 + 3 * NEWTONS

            def bias_columns():
                dve.wait_ge(cols_in_psum, 1)
                nc.vector.tensor_copy(bias_cols[:, :], b_t[:, 0:3]).then_inc(cols_ready, 1)
                nc.vector.tensor_copy(w1v[:, :, FF:W1C],
                                      b_t[:, 3:NROWS].rearrange("p (e c) -> p e c", e=E)
                                      ).then_inc(cols_ready, 1)

            def step(i, c):
                s = 2 * i + c
                par, odd = c % 2, (c + 1) % 2

                def x_stats(js):
                    g = s + 3
                    if live(g):
                        for j in js:
                            op = nc.vector.bn_stats(stats[:, odd, j, :], graph(x_res, g * G + j))
                            if j == G - 1:
                                op.then_inc(stats1_done, 1)

                lo, hi = ln_columns(s)

                def refine(n):
                    if not chained(s):
                        return
                    y, t, v = rough[:, lo:hi], newton_t[:, lo:hi], var_eps[:, lo:hi]
                    if n == 0:
                        dve.wait_ge(guess_ready, s + 3)
                        nc.vector.tensor_tensor(t, y, y, ALU.mult).then_inc(ln_chain, 1)
                    elif n == 1:
                        dve.wait_ge(ln_chain, CHAIN1 * (s + 2) + 3)
                        nc.vector.scalar_tensor_tensor(t, t, -0.5, v, ALU.mult,
                                                       ALU.mult).then_inc(ln_chain, 1)
                    else:
                        dve.wait_ge(ln_chain, CHAIN1 * (s + 2) + 4)
                        nc.vector.scalar_tensor_tensor(rstd[:, par, lo:hi], t, 1.5, y, ALU.add,
                                                       ALU.mult).then_inc(ln_ready, 1)

                if live(s + 2):
                    dve.wait_ge(stats1_done, s + 3)
                    wait(dve, xn_ready, s + 1)
                if live(s - 3):
                    dve.wait_ge(stats2_done, s - 2)
                if chained(s):
                    wait(dve, xl_ready, s - 4)
                if live(s + 3):
                    dve.wait_ge(x_in[odd], 16 * (i + (c + 3) // 2 + 1))
                g = s - 2
                if live(g):
                    wait(dve, rel_ready, g - 1)
                    dve.wait_ge(prob_ready, g + 1)
                    nc.vector.reciprocal(rden[:, par, :], den[:, par, :]).then_inc(rden_ready, 1)
                if chained(s):
                    for j in range(lo, hi):
                        op = nc.vector.bn_aggr(mv[:, par, j, :], stats[:, par, j, :])
                    op.then_inc(ln_chain, 1)
                x_stats((0,))
                if chained(s):
                    dve.wait_ge(ln_chain, CHAIN1 * (s + 2) + 1)
                    nc.vector.tensor_scalar(var_eps[:, lo:hi], mv[:, par, lo:hi, 1], LN_EPS, None,
                                            ALU.add).then_inc(ln_chain, 1)
                    nc.vector.tensor_scalar(neg_mean[:, par, lo:hi], mv[:, par, lo:hi, 0], -1.0,
                                            None, ALU.mult)
                g = s - 1
                if live(g):
                    wait(dve, y_in_psum, g - 1)
                    if isinstance(g, int) and g == 0:
                        dve.wait_ge(gnn_w_in, 16 * 5)
                    dve.wait_ge(vw_in_psum, g + 1)
                    nc.vector.tensor_tensor(by_graph(vw[:, odd, :]), by_graph(b_w[:, :]),
                                            repeat(bo_bc[:, :], G), ALU.add).then_inc(vw_ready, 1)
                x_stats((1,))
                if live(g):
                    dve.wait_ge(adj_in[odd], 16 * (i + (c - 1) // 2 + 1))
                    wait(dve, prob_ready, g)
                    dve.wait_ge(scores_in_psum, g + 1)
                    nc.vector.tensor_tensor(score[:, :], b_s[:, :], adj_sb[:, odd, :],
                                            ALU.mult).then_inc(scores_masked, 1)
                x_stats((2,))
                refine(0)
                x_stats((3,))
                refine(1)
                refine(2)
                if live(g):
                    wait(dve, prob_ready, g - 1)
                    dve.wait_ge(score_ready, g + 1)
                    nc.vector.tensor_reduce(neg_max[:, odd, :], by_graph(score[:, :]), AX.X,
                                            ALU.max, negate=True).then_inc(max_ready, 1)
                g = s - 2
                if live(g):
                    dve.wait_ge(rel_ready, g + 1)
                    nc.vector.tensor_tensor(group(x_res, g), group(x_res, g), rel[:, :],
                                            ALU.add).then_inc(x1_ready, 1)
                    dve.wait_ge(x1_ready, g + 1)
                g = s - 5
                if live(g):
                    dve.wait_ge(xlT_ready, g + 1)
                    nc.vector.tensor_reduce(mean_sum[:, bass.ds(g * G, G)],
                                            by_graph(group(xlT_res, g)),
                                            AX.X, ALU.add).then_inc(mean_done, 1)
                g = s - 2
                if live(g):
                    for j in range(G):
                        op = nc.vector.bn_stats(stats[:, odd, G + j, :], graph(x_res, g * G + j))
                    op.then_inc(stats2_done, 1)

            step(0, -3)
            bias_columns()
            run_steps(dve, step, -2, 6, 12, GROUPS + 5)

            count = [0]

            def then(op):
                count[0] += 1
                op.then_inc(route_dve, 1)
                dve.wait_ge(route_dve, count[0])

            def columns(n):
                return r1[:, n:n + 1]

            vec = nc.vector
            dve.wait_ge(route_pe, 1)
            dve.wait_ge(late_w_in, 16 * 5)
            then(vec.scalar_tensor_tensor(rt[:, 0, :], b_s[0:GRAPHS, 0:E], 1.0 / NODES,
                                          br_bc[:, :], ALU.mult, ALU.add))
            then(vec.tensor_reduce(columns(0), rt[:, 0, :], AX.X, ALU.max, negate=True))
            dve.wait_ge(route_act, 1)
            then(vec.reciprocal(columns(2), columns(1)))
            then(vec.tensor_scalar(rt[:, 2, :], rt[:, 1, :], columns(2), None, ALU.mult))
            dve.wait_ge(route_pe, 2)
            then(vec.tensor_scalar(rt[:, 3, :], b_s[0:GRAPHS, E:2 * E], float(NODES), None, ALU.mult))
            then(vec.reciprocal(rt[:, 6, :], rt[:, 3, :]))
            then(vec.tensor_scalar(rt[:, 7, :], rt[:, 6, :], CAPACITY, 1.0, ALU.mult, ALU.min))
            then(vec.tensor_tensor(rt[:, 4, :], rt[:, 2, :], rt[:, 7, :], ALU.mult))
            then(vec.tensor_reduce(columns(3), rt[:, 4, :], AX.X, ALU.max, negate=True))
            dve.wait_ge(route_act, 2)
            then(vec.reciprocal(columns(5), columns(4)))
            then(vec.tensor_scalar(rt[:, 8, :], rt[:, 5, :], columns(5), None, ALU.mult))
            then(vec.max(rt[:, 9, :], rt[:, 8, :]))
            then(vec.max_index(top_at[:, :], rt[:, 9, :], rt[:, 8, :]))
            then(vec.tensor_tensor(columns(6), rt[:, 9, 1:2], rt[:, 9, 0:1], ALU.subtract))
            then(vec.tensor_copy(picked[:, TOP:2 * TOP], top_at[:, 0:TOP]))
            dve.wait_ge(route_act, 3)
            then(vec.tensor_scalar(columns(8), columns(7), 1.0, None, ALU.add))
            then(vec.reciprocal(picked[:, 0:1], columns(8)))
            then(vec.tensor_tensor(picked[:, 1:2], picked[:, 0:1], columns(7), ALU.mult))
            dve.wait_ge(const_ready, 2)
            dve.wait_ge(ident_ready, 1)
            then(vec.tensor_tensor(picked_diag[:, :, :], repeat(ident[0:GRAPHS, 0:GRAPHS], 2 * TOP),
                                   picked[:, :].unsqueeze(2).broadcast_to([GRAPHS, 2 * TOP, GRAPHS]),
                                   ALU.mult))
            for k in range(TOP):
                then(vec.tensor_scalar(rt[:, 10 + k, :], iota_e[:, :], picked[:, TOP + k:TOP + k + 1],
                                       picked[:, k:k + 1], ALU.is_equal, ALU.mult))
            then(vec.tensor_tensor(rt[:, 12, :], rt[:, 10, :], rt[:, 11, :], ALU.add))
            dve.wait_ge(route_pe, 3)
            for table, stride in ((w1_at, W1C), (w2_at, FC * D)):
                vec.tensor_scalar(table[:, :].rearrange("p (b k) -> p b k", k=TOP),
                                  b_t[0:1, TOP * GRAPHS:2 * TOP * GRAPHS]
                                  .rearrange("p (k b) -> p b k", k=TOP), float(stride), None,
                                  ALU.mult).then_inc(experts_ready, 1)
            vec.tensor_copy(w_bc[:, :, :], b_t[:, 0:TOP * GRAPHS]
                            .rearrange("p (k b) -> p k b", k=TOP)).then_inc(experts_ready, 1)
            dve.wait_ge(route_pe, 4)
            vec.tensor_copy(denseT[:, :], b_s[0:E, 0:GRAPHS]).then_inc(route_dve, 1)
            dve.wait_ge(route_pe, 5)
            vec.tensor_copy(bias2[:, :], b_y[0:GRAPHS, 0:D]).then_inc(bias2_ready, 1)
            dve.wait_ge(experts_ready, 3)

            def z_of(g, j, k):
                b = g * G + j
                by = y_banks[j]
                at = k * D
                if k == 0:
                    dve.wait_ge(e_in_psum, b + 1)
                    if j == 0:
                        dve.wait_ge(res_ready, g + 1)
                else:
                    dve.wait_ge(z0_done, b + 1)
                vec.scalar_tensor_tensor(graph(xl_res, b), by[:, at:at + D],
                                         w_bc[:, k, bass.ds(b, 1)], graph(xl_res, b),
                                         ALU.mult, ALU.add).then_inc((z0_done, z_done)[k], 1)

            def z_stats(b, j):
                vec.bn_stats(stats[:, 0, j, :], graph(xl_res, b)).then_inc(zstats_done, 1)

            def aggregate(g):
                for j in range(G):
                    op = vec.bn_aggr(mv[:, 0, j, :], stats[:, 0, j, :])
                op.then_inc(ln2_chain, 1)

            def chain_op(g, n):
                base = CHAIN2 * g
                if n < 0:
                    dve.wait_ge(ln2_chain, base + 1)
                    vec.tensor_scalar(var_eps[:, 0:G], mv[:, 0, 0:G, 1], LN_EPS, None,
                                      ALU.add).then_inc(ln2_chain, 1)
                elif n < RSQRT_OPS:
                    if n == RSQRT_OPS - 1:
                        wait(dve, unit_ready, g)
                    rsqrt_op(n, ln2_chain, base + 1, 0, G, rstd[:, 0, 0:G], ln2_chain)
                else:
                    dve.wait_ge(ln2_chain, base + RSQRT_OPS + 2)
                    vec.scalar_tensor_tensor(neg_mr[:, :], mv[:, 0, 0:G, 0], -1.0, rstd[:, 0, 0:G],
                                             ALU.mult, ALU.mult).then_inc(ln2_ready, 1)

            def final(g, part):
                u, x1 = by_graph(group(xl_res, g)), by_graph(group(x_res, g))
                if part == 0:
                    dve.wait_ge(unit_ready, g + 1)
                    vec.tensor_tensor(u, u, repeat(gamma_bc[:, :], G), ALU.mult).then_inc(scaled, 1)
                elif part == 1:
                    vec.tensor_tensor(x1, x1, repeat(beta_bc[:, :], G), ALU.add).then_inc(shifted, 1)
                else:
                    dve.wait_ge(scaled, g + 1)
                    dve.wait_ge(shifted, g + 1)
                    vec.tensor_tensor(x1, x1, u, ALU.add).then_inc(final_ready, 1)

            def group_step(g, zs, chain, finals):
                if chain:
                    dve.wait_ge(zstats_done, g * G)
                n = -1
                for j in range(G):
                    if zs:
                        z_of(g, j, 0)
                    if chain and j == 0:
                        aggregate(g - 1)
                    if zs and j > 0:
                        dve.wait_ge(z_done, g * G + j)
                    if chain:
                        chain_op(g - 1, n)
                    if zs and j > 0:
                        z_stats(g * G + j - 1, j - 1)
                    if chain:
                        chain_op(g - 1, n + 1)
                    if zs:
                        z_of(g, j, 1)
                    if chain and n + 2 < RSQRT_OPS + 1:
                        chain_op(g - 1, n + 2)
                    n += 3
                    if finals and j in (1, 2):
                        final(g - 3, j - 1)
                if chain:
                    for n in range(n, RSQRT_OPS + 1):
                        chain_op(g - 1, n)
                if zs:
                    dve.wait_ge(z_done, g * G + G)
                if finals:
                    final(g - 3, 2)
                if zs:
                    z_stats(g * G + G - 1, G - 1)

            group_step(0, True, False, False)
            group_step(1, True, True, False)
            group_step(2, True, True, False)
            with dve.Fori(3, GROUPS) as g:
                group_step(g, True, True, True)
            group_step(GROUPS, False, True, True)
            group_step(GROUPS + 1, False, False, True)
            group_step(GROUPS + 2, False, False, True)

        @block.tensor
        def _(pe):
            pe.wait_ge(ident_ready, 1)
            pe.wait_ge(rows_in, 16 * 4)
            nc.tensor.transpose(b_t[:, 0:NROWS], bias_rows[:, :],
                                ident[0:NROWS, 0:NROWS]).then_inc(cols_in_psum, 1)
            pe.wait_ge(cols_ready, 2)
            pe.wait_ge(gnn_w_in, 16 * 5)

            def transposes(dst, src, done):
                for j in range(G):
                    op = nc.tensor.transpose(dst[:, j * P:(j + 1) * P], src[:, j * P:(j + 1) * P],
                                             ident[:, :])
                op.then_inc(done, 1)

            def products(dst, left, right, done):
                for j in range(G):
                    cut = slice(j * P, (j + 1) * P)
                    op = nc.tensor.matmul(dst[:, cut], left[:, cut],
                                          right[:, cut] if right.shape[-1] == GD else right,
                                          start=True, stop=True)
                op.then_inc(done, 1)

            def step(i, c):
                s = 2 * i + c
                g = s
                if live(g):
                    pe.wait_ge(xn_ready, g + 1)
                    wait(pe, xlT_ready, g - 4)
                    transposes(b_t, xn[:, c % 2, :], xnT_in_psum)
                g = s - 1
                if live(g):
                    pe.wait_ge(q_ready, g + 1)
                    pe.wait_ge(k_ready, g + 1)
                    wait(pe, scores_masked, g)
                    products(b_s, qT, kT, scores_in_psum)
                    pe.wait_ge(v_ready, g + 1)
                    wait(pe, vw_ready, g)
                    products(b_w, vT, wo_sb[:, :], vw_in_psum)
                g = s - 2
                if live(g):
                    pe.wait_ge(prob_ready, g + 1)
                    wait(pe, probT_ready, g)
                    transposes(b_p, prob, probT_in_psum)
                g = s - 4
                if live(g):
                    pe.wait_ge(xl_ready, g + 1)
                    if live(s):
                        wait(pe, xnT_ready, s + 1)
                    else:
                        wait(pe, xlT_ready, g)
                    transposes(b_t, xl[:, c % 2, :], xlT_in_psum)

                def project(w, dst, done, free):
                    if live(s):
                        pe.wait_ge(xnT_ready, s + 1)
                        wait(pe, free, s)
                        nc.tensor.matmul(dst[:, :], w[:, :], xnT[:, :], start=True,
                                         stop=True).then_inc(done, 1)

                project(wq_sb, b_q, q_in_psum, q_ready)
                g = s - 2
                if live(g):
                    pe.wait_ge(probT_ready, g + 1)
                    pe.wait_ge(vw_ready, g + 1)
                    wait(pe, rel_ready, g)
                    products(b_y, probT, vw[:, c % 2, :], y_in_psum)
                project(wk_sb, b_k, k_in_psum, k_ready)
                project(wv_sb, b_v, v_in_psum, v_ready)
            run_steps(pe, step, 0, 6, 16, GROUPS + 4)

            pe.wait_ge(mean_done, GROUPS)
            pe.wait_ge(late_w_in, 16 * 5)
            pe.wait_ge(const_ready, 2)
            nc.tensor.matmul(b_s[0:GRAPHS, 0:E], mean_sum[:, :], wr_sb[:, :], start=True,
                             stop=True).then_inc(route_pe, 1)
            pe.wait_ge(route_dve, 4)
            nc.tensor.matmul(b_s[0:GRAPHS, E:2 * E], ones[0:GRAPHS, 0:GRAPHS], rt[:, 2, :],
                             start=True, stop=True).then_inc(route_pe, 1)
            pe.wait_ge(route_dve, 19)
            nc.tensor.matmul(b_t[:, 0:2 * TOP * GRAPHS], ones[0:GRAPHS, 0:P],
                             picked_diag[:, :, :].rearrange("b q c -> b (q c)"), start=True,
                             stop=True).then_inc(route_pe, 1)
            pe.wait_ge(route_dve, 22)
            nc.tensor.transpose(b_s[0:E, 0:GRAPHS], rt[:, 12, :],
                                ident[0:GRAPHS, 0:GRAPHS]).then_inc(route_pe, 1)
            pe.wait_ge(route_dve, 23)
            nc.tensor.matmul(b_y[0:GRAPHS, 0:D], denseT[:, :], b2_sb[:, :], start=True,
                             stop=True).then_inc(route_pe, 1)

            pe.wait_ge(w2_in, 16)
            pe.wait_ge(experts_ready, 3)
            pe.wait_ge(bias2_ready, 1)
            pe.wait_ge(xlT_ready, GROUPS)

            def hidden(g, j):
                b = g * G + j
                pe.wait_ge(w1_picked, b + 1)
                wait(pe, gelu_done, b - G + 1)
                for k in range(TOP):
                    for f in range(FC):
                        at = (k * FC + f) * P
                        op = nc.tensor.matmul(h_banks[j][:, at:at + P],
                                              w1_pick[:, j, k, f * P:(f + 1) * P],
                                              graph(xlT_res, b), start=True, stop=True)
                op.then_inc(h_in_psum, 1)

            def experts(b, j, at):
                pe.wait_ge(gelu_done, b + 1)
                wait(pe, z_done, b - G + 1)
                for k in range(TOP):
                    for f in range(FC):
                        op = nc.tensor.matmul(y_banks[j][:, k * D:(k + 1) * D],
                                              hT[:, j, (k * FC + f) * P:(k * FC + f + 1) * P],
                                              w2_sb[:, bass.ds(at[k] + f * D, D)],
                                              start=(f == 0), stop=(f == FC - 1))
                op.then_inc(e_in_psum, 1)

            LAG = 2

            def group_step(g, lagging):
                first = 0 if lagging else LAG
                at = places(mybir.EngineType.PE, w2_at, g * G + first - LAG, G - first, FC * D)
                for j in range(G):
                    hidden(g, j)
                    if j >= first:
                        n = TOP * (j - first)
                        experts(g * G + j - LAG, (j - LAG) % G, at[n:n + TOP])

            group_step(0, False)
            group_step(1, True)
            with pe.Fori(2, GROUPS) as g:
                group_step(g, True)
            at = places(mybir.EngineType.PE, w2_at, GRAPHS - LAG, LAG, FC * D)
            for n in range(LAG):
                experts(GRAPHS - LAG + n, G - LAG + n, at[n * TOP:(n + 1) * TOP])


_INS = ["x", "adj", "L0_gnn_Wv", "L0_gnn_bv", "L0_gnn_Wk", "L0_gnn_bk", "L0_gnn_Wq", "L0_gnn_bq",
        "L0_gnn_Wo", "L0_gnn_bo", "L0_ffn_Wr", "L0_ffn_br", "L0_ffn_W1", "L0_ffn_b1", "L0_ffn_W2",
        "L0_ffn_b2", "L0_ffn_gamma", "L0_ffn_beta"]


def kernel(**inputs):
    import numpy as np
    import concourse.bacc as bacc
    from concourse.bass_utils import run_bass_kernel_spmd

    nc = bacc.Bacc("TRN2", target_bir_lowering=False, num_devices=1)
    arrays, args = {}, []
    for name in _INS:
        a = np.ascontiguousarray(inputs[name])
        arrays["in_" + name] = a
        args.append(nc.dram_tensor("in_" + name, a.shape, mybir.dt.from_np(a.dtype),
                                   kind="ExternalInput").ap())
    result = nc.dram_tensor("out_0", inputs["x"].shape, F32, kind="ExternalOutput").ap()
    build(nc, *args, result)
    r = run_bass_kernel_spmd(nc, [arrays], core_ids=[0])
    return r.results[0]["out_0"]
```

```python
from contextlib import ExitStack

import concourse.bass as bass
from concourse import mybir

F32 = mybir.dt.float32
I32 = mybir.dt.int32
U32 = mybir.dt.uint32
ALU = mybir.AluOpType
ACT = mybir.ActivationFunctionType
AX = mybir.AxisListType

P = 128
G = 4
TOP = 2
NEG = 9000000000000000.0
LN_EPS = 1e-5
RSQRT_MAGIC = float(0x5F3759DF)
NEWTONS = 3
CHAIN1 = 4
CHAIN2 = 4 + 3 * NEWTONS
STORE_LAG = 5
WARM = (9, 3, 11, 4, 2, 1)
CAPACITY_FACTOR = 1.25


def wait(engine, semaphore, value):
    if not isinstance(value, int) or value > 0:
        engine.wait_ge(semaphore, value)


def is_last(i, n):
    return isinstance(i, int) and i == n - 1


def after(engine, semaphore, i, value=1):
    if not isinstance(i, int):
        engine.wait_ge(semaphore, value)


def run_steps(engine, body, first, loop_from, loop_to, end):
    for s in range(first, loop_from):
        body(0, s)
    with engine.Fori(loop_from // 2, loop_to // 2) as i:
        body(i, 0)
        body(i, 1)
    for s in range(loop_to, end):
        body(0, s)


def build(nc, x, adj, Wv, bv, Wk, bk, Wq, bq, Wo, bo, Wr, br, W1, b1, W2, b2, gamma, beta, out):
    GRAPHS, NODES, D = x.shape
    E, _, FF = W1.shape
    FC = FF // P
    GROUPS = GRAPHS // G
    GD = G * D
    W1C = FF + FC
    CAPACITY = float(-(-GRAPHS * NODES * CAPACITY_FACTOR // E))
    assert NODES == P and D == P and FF % P == 0 and GRAPHS % (2 * G) == 0

    def live(g):
        return not isinstance(g, int) or 0 <= g < GROUPS

    def chained(s):
        return live(s + 2) or live(s - 3)

    def ln_columns(s):
        return 0 if live(s + 2) else G, 2 * G if live(s - 3) else G

    GUESSES = sum(chained(s) for s in range(-3, GROUPS + 5))

    bias2_dram = nc.dram_tensor("bias2_scratch", (GRAPHS, D), F32).ap()

    ctx = ExitStack()
    with ctx:
        def sb(name, shape, dt=F32):
            return ctx.enter_context(nc.sbuf_tensor(name, shape, dt))

        def bank(name):
            return ctx.enter_context(nc.psum_tensor(name, [P, GD], F32))

        def sem(name):
            return ctx.enter_context(nc.semaphore(name))

        x_res = sb("x_res", [P, GRAPHS * D])
        xl_res = sb("xl_res", [P, GRAPHS * D])
        xlT_res = sb("xlT_res", [P, GRAPHS * P])
        b2bc = sb("b2bc", [P, GRAPHS * D])
        w1_sb = sb("w1_sb", [P, E * W1C])
        w1v = w1_sb[:, :].rearrange("p (e c) -> p e c", e=E)
        w2_sb = sb("w2_sb", [P, E * FC * D])
        wq_sb, wk_sb, wv_sb, wo_sb = (sb(n, [P, D]) for n in ("wq_sb", "wk_sb", "wv_sb", "wo_sb"))
        wr_sb = sb("wr_sb", [P, E])
        bo_bc = sb("bo_bc", [P, D])
        gamma_bc = sb("gamma_bc", [P, D])
        beta_bc = sb("beta_bc", [P, D])
        br_bc = sb("br_bc", [GRAPHS, E])
        b2_sb = sb("b2_sb", [E, D])
        NROWS = 3 + E * FC
        bias_rows = sb("bias_rows", [NROWS, P])
        bias_cols = sb("bias_cols", [P, 3])
        ident = sb("ident", [P, P])
        ones = sb("ones", [P, W1C])

        adj_sb = sb("adj_sb", [P, 2, GD])
        xn = sb("xn", [P, 2, GD])
        xnT = sb("xnT", [P, GD])
        qT = sb("qT", [P, GD])
        kT = sb("kT", [P, GD])
        vT = sb("vT", [P, GD])
        vw = sb("vw", [P, 2, GD])
        neg_mask = sb("neg_mask", [P, GD])
        score = sb("score", [P, GD])
        prob = sb("prob", [P, GD])
        probT = sb("probT", [P, GD])
        rel = sb("rel", [P, GD])
        xl = sb("xl", [P, 2, GD])
        neg_max = sb("neg_max", [P, 2, G])
        den = sb("den", [P, 2, G])
        rden = sb("rden", [P, 2, G])
        mean_sum = sb("mean_sum", [P, GRAPHS])
        stats = sb("stats", [P, 2, 2 * G, 6])
        mv = sb("mv", [P, 2, 2 * G, 2])
        neg_mean = sb("neg_mean", [P, 2, 2 * G])
        rstd = sb("rstd", [P, 2, 2 * G])
        var_eps = sb("var_eps", [P, 2 * G])
        halved = sb("halved", [P, 2 * G], I32)
        guess = sb("guess", [P, 2 * G], I32)
        log_var = sb("log_var", [P, 2 * G])
        rough = sb("rough", [P, 2 * G])
        newton_y = sb("newton_y", [P, 2 * G])
        newton_t = sb("newton_t", [P, 2 * G])

        rt = sb("rt", [GRAPHS, 16, E])
        r1 = sb("r1", [GRAPHS, 16])
        top_at = sb("top_at", [GRAPHS, E], U32)
        picked = sb("picked", [GRAPHS, 2 * TOP])
        picked_diag = sb("picked_diag", [GRAPHS, 2 * TOP, GRAPHS])
        w_bc = sb("w_bc", [P, TOP, GRAPHS])
        w1_at = sb("w1_at", [1, GRAPHS * TOP], I32)
        w2_at = sb("w2_at", [1, GRAPHS * TOP], I32)
        iota_e = sb("iota_e", [GRAPHS, E])
        denseT = sb("denseT", [E, GRAPHS])
        bias2 = sb("bias2", [GRAPHS, D])

        w1_pick = sb("w1_pick", [P, G, TOP, W1C])
        hT = sb("hT", [P, G, TOP * FC * P])
        neg_mr = sb("neg_mr", [P, 2, G])

        b_p, b_t, b_s, b_y, b_q, b_k, b_v, b_w = (bank("bank_" + n) for n in "ptsyqkvw")
        h_banks, y_banks = (b_q, b_k, b_p, b_y), (b_v, b_w, b_s, b_t)

        x_in = [sem(f"x_in{n}") for n in range(2)]
        adj_in = [sem(f"adj_in{n}") for n in range(2)]
        qkv_w_in, wo_in, rows_in, late_w_in, w1_in, w2_in = (
            sem(n) for n in ("qkv_w_in", "wo_in", "rows_in", "late_w_in", "w1_in", "w2_in"))
        zeroed, ident_ready, const_ready = sem("zeroed"), sem("ident_ready"), sem("const_ready")
        cols_in_psum, cols_ready = sem("cols_in_psum"), sem("cols_ready")
        stats1_done, stats2_done = sem("stats1_done"), sem("stats2_done")
        centred = [sem("xn_centred"), sem("xl_centred")]
        ln_chain, log_ready, guess_ready, ln_ready = (
            sem("ln_chain"), sem("log_ready"), sem("guess_ready"), sem("ln_ready"))
        xn_ready, xnT_in_psum, xnT_ready = sem("xn_ready"), sem("xnT_in_psum"), sem("xnT_ready")
        q_in_psum, k_in_psum, v_in_psum = sem("q_in_psum"), sem("k_in_psum"), sem("v_in_psum")
        q_ready, k_ready, v_ready = sem("q_ready"), sem("k_ready"), sem("v_ready")
        vw_in_psum, vw_ready = sem("vw_in_psum"), sem("vw_ready")
        scores_in_psum, scores_masked = sem("scores_in_psum"), sem("scores_masked")
        neg_mask_ready, score_ready, max_ready = (
            sem("neg_mask_ready"), sem("score_ready"), sem("max_ready"))
        prob_ready, probT_in_psum, probT_ready = (
            sem("prob_ready"), sem("probT_in_psum"), sem("probT_ready"))
        rden_ready, y_in_psum, rel_ready, x1_ready = (
            sem("rden_ready"), sem("y_in_psum"), sem("rel_ready"), sem("x1_ready"))
        xl_ready, xlT_in_psum, xlT_ready, mean_done = (
            sem("xl_ready"), sem("xlT_in_psum"), sem("xlT_ready"), sem("mean_done"))
        last_score_ready, last_xl_ready = sem("last_score_ready"), sem("last_xl_ready")
        mean_in_psum = sem("mean_in_psum")
        xl_saved = [sem(f"xl_saved{n}") for n in range(2)]
        route_pe, route_dve, route_act = sem("route_pe"), sem("route_dve"), sem("route_act")
        experts_ready = sem("experts_ready")
        bias2_ready, bias2_out = sem("bias2_ready"), sem("bias2_out")
        bias2_in = [sem(f"bias2_in{n}") for n in range(2)]
        w1_picked = sem("w1_picked")
        w1_moved = [sem(f"w1_moved{j}") for j in range(2)]
        h_in_psum, gelu_done, e_in_psum = sem("h_in_psum"), sem("gelu_done"), sem("e_in_psum")
        res_ready, first_res_in_psum, first_res_ready = (
            sem("group_res_ready"), sem("first_res_in_psum"), sem("first_res_ready"))
        z0_done, z_done, zstats_done = sem("z0_done"), sem("z_done"), sem("zstats_done")
        ln2_chain, ln2_ready, unit_ready = (
            sem("ln2_chain"), sem("group_ln2_ready"), sem("group_unit_ready"))
        scaled, shifted, final_ready, out_done = (
            sem("group_scaled"), sem("group_shifted"), sem("group_final_ready"), sem("out_done"))
        last_unit, last_scaled, last_final_ready = (
            sem("last_unit"), sem("last_scaled"), sem("last_final_ready"))

        def group(tensor, g):
            return tensor[:, bass.ds(g * GD, GD)]

        def graph(tensor, b):
            return tensor[:, bass.ds(b * D, D)]

        def places(engine, table, first, graphs, stride):
            at = table[0:1, bass.ds(first * TOP, graphs * TOP)]
            _, values = nc.values_load_multi_w_load_instructions(
                at, engines=[engine], min_val=0, max_val=(E - 1) * stride,
                skip_runtime_bounds_check_because="top-2 of E experts")
            return values

        def by_graph(ap):
            return ap.rearrange("p (g n) -> p g n", g=G)

        def repeat(ap, times):
            return ap.unsqueeze(1).broadcast_to([ap.shape[0], times, ap.shape[1]])

        block = ctx.enter_context(nc.Block())

        @block.sync
        def _(sp):
            x_v = x.rearrange("b n d -> n b d")
            adj_v = adj.rearrange("b n m -> n b m")

            def load_x(i):
                for n in range(2):
                    wait(sp, x_in[n], 16 * i)
                    after(sp, x_in[n], i, 16)
                    sp.dma_start(by_graph(group(x_res, 2 * i + n)),
                                 x_v[:, bass.ds((2 * i + n) * G, G), :]).then_inc(x_in[n], 16)

            def save_xl(g, n):
                wait(sp, xl_ready, g + 1)
                after(sp, xl_ready, g)
                sp.dma_start(group(xl_res, g), xl[:, n, :]).then_inc(xl_saved[n], 16)

            def load_adj(i, saving=False):
                for n in range(2):
                    g = 2 * i + n
                    wait(sp, adj_in[n], 16 * i)
                    wait(sp, neg_mask_ready, g - 1)
                    wait(sp, scores_masked, g - 1)
                    after(sp, adj_in[n], i, 16)
                    sp.dma_start(by_graph(adj_sb[:, n, :]),
                                 adj_v[:, bass.ds(g * G, G), :]).then_inc(adj_in[n], 16)
                    if saving:
                        save_xl(g - 4, n)

            load_x(0)
            load_adj(0)
            load_x(1)
            sp.dma_start(wo_sb[:, :], Wo).then_inc(wo_in, 16)
            sp.dma_start(bo_bc[:, :], bo.unsqueeze(0).broadcast_to([P, D])).then_inc(wo_in, 16)
            load_x(2)
            load_x(3)
            load_adj(1)
            sp.dma_start(wr_sb[:, :], Wr).then_inc(late_w_in, 16)
            sp.dma_start(br_bc[:, :], br.unsqueeze(0).broadcast_to([GRAPHS, E])).then_inc(late_w_in, 16)
            sp.dma_start(b2_sb[:, :], b2).then_inc(late_w_in, 16)
            for dst, src in ((gamma_bc, gamma), (beta_bc, beta)):
                sp.dma_start(dst[:, :], src.unsqueeze(0).broadcast_to([P, D])).then_inc(late_w_in, 16)
            with sp.Fori(2, GROUPS // 2 - 2) as i:
                load_x(i + 2)
                load_adj(i, True)
            load_adj(GROUPS // 2 - 2, True)
            load_adj(GROUPS // 2 - 1, True)
            sp.dma_start(w1v[:, :, 0:FF], W1.rearrange("e d f -> d e f")).then_inc(w1_in, 16)
            sp.dma_start(w2_sb[:, :].rearrange("p (e c d) -> p e c d", e=E, c=FC),
                         W2.rearrange("e (c p) d -> p e c d", p=P)).then_inc(w2_in, 16)
            for n in range(2):
                save_xl(GROUPS - 4 + n, n)
            for n, ready, count in ((0, xl_ready, GROUPS - 1), (1, last_xl_ready, 1)):
                sp.wait_ge(ready, count)
                sp.dma_start(group(xl_res, GROUPS - 2 + n), xl[:, n, :]).then_inc(xl_saved[n], 16)
            sp.wait_ge(experts_ready, 1)
            sp.wait_ge(w1_in, 16)
            sp.wait_ge(cols_ready, 2)

            def pick(g, j):
                at = places(mybir.EngineType.SP, w1_at, g * G + j, 1, W1C)
                wait(sp, gelu_done, (g - 1) * G + j + 1)
                after(sp, gelu_done, g)
                for k in range(TOP):
                    sp.dma_start(w1_pick[:, j, k, :], w1_sb[:, bass.ds(at[k], W1C)]
                                 ).then_inc(w1_moved[j // (G - 1)], 16)

            bias2_v = bias2_dram.rearrange("(g b) d -> g (b d)", b=G)

            def load_bias2(g, n):
                sp.dma_start(group(b2bc, g), bias2_v[bass.ds(g, 1), :]
                             .broadcast_to([P, GD])).then_inc(bias2_in[n], 16)

            out_v = out.rearrange("b n d -> n b d")

            def store(g):
                sp.wait_ge(final_ready, g + 1)
                after(sp, final_ready, g)
                sp.dma_start(out_v[:, bass.ds(g * G, G), :],
                             by_graph(group(x_res, g))).then_inc(out_done, 16)

            def group_step(i, c):
                g = 2 * i + c
                if live(g):
                    pick(g, 0)
                if live(g + 1):
                    wait(sp, bias2_in[(c + 1) % 2], 16 * (i + c // 2))
                    after(sp, bias2_in[(c + 1) % 2], i, 16)
                    load_bias2(g + 1, (c + 1) % 2)
                if live(g - STORE_LAG):
                    store(g - STORE_LAG)
                if live(g):
                    pick(g, G - 1)

            pick(0, G - 1)
            sp.wait_ge(bias2_ready, 1)
            sp.dma_start(bias2_dram, bias2[:, :]).then_inc(bias2_out, 16)
            sp.wait_ge(bias2_out, 16)
            load_bias2(1, 1)
            run_steps(sp, group_step, 1, 6, GROUPS - 2, GROUPS - 1 + STORE_LAG)
            for n in (1, 0):
                lo = GRAPHS - G + n * G // 2
                sp.wait_ge(last_final_ready, 2 - n)
                sp.dma_start(out_v[:, lo:lo + G // 2, :],
                             x_res[:, lo * D:(lo + G // 2) * D]
                             .rearrange("p (g n) -> p g n", g=G // 2)).then_inc(out_done, 16)
            sp.wait_ge(out_done, 16 * (GROUPS + 1))

        @block.gpsimd
        def _(pool):
            nc.gpsimd.memset(ident[:, :], 0.0).then_inc(zeroed, 1)
            nc.gpsimd.memset(ones[:, :], 1.0).then_inc(const_ready, 1)
            nc.gpsimd.iota(iota_e[:, :], pattern=[[1, E]], base=0, channel_multiplier=0,
                           allow_small_or_imprecise_dtypes=True).then_inc(const_ready, 1)
            pool.wait_ge(zeroed, 1)
            nc.gpsimd.affine_select(out=ident[:, :], in_=ident[:, :], compare_op=ALU.not_equal,
                                    fill=1.0, base=0, pattern=[[-1, P]],
                                    channel_multiplier=1).then_inc(ident_ready, 1)
            for dst, src in ((wq_sb, Wq), (wk_sb, Wk), (wv_sb, Wv)):
                pool.dma_start(dst[:, :], src).then_inc(qkv_w_in, 16)

            def normalise(dst, g, par, ln, ready):
                def each(ap):
                    return ap[:, par, ln * G:(ln + 1) * G].unsqueeze(2).broadcast_to([P, G, D])

                nc.gpsimd.tensor_tensor(by_graph(dst), by_graph(group(x_res, g)), each(neg_mean),
                                        ALU.add).then_inc(centred[ln], 1)
                wait(pool, centred[ln], g + 1)
                nc.gpsimd.tensor_tensor(by_graph(dst), by_graph(dst), each(rstd),
                                        ALU.mult).then_inc(ready, 1)

            def step(i, c):
                s = 2 * i + c
                g = s - 1
                if live(g) and not is_last(g, GROUPS):
                    wait(pool, scores_masked, g + 1)
                    wait(pool, neg_mask_ready, g + 1)
                    nc.gpsimd.tensor_tensor(score[:, :], score[:, :], neg_mask[:, :],
                                            ALU.add).then_inc(score_ready, 1)
                g = s + 1
                if live(g):
                    wait(pool, ln_ready, g + 1)
                    wait(pool, xnT_in_psum, g - 1)
                    normalise(xn[:, (c + 1) % 2, :], g, (c + 1) % 2, 0, xn_ready)
                if live(s):
                    pool.wait_ge(adj_in[c % 2], 16 * (i + c // 2 + 1))
                    wait(pool, score_ready, s)
                g = s - 3
                if live(g) and not is_last(g, GROUPS):
                    wait(pool, ln_ready, g + 6)
                    wait(pool, xlT_in_psum, g - 1)
                    wait(pool, xl_saved[(c + 1) % 2], 16 * (i + (c - 3) // 2))
                    normalise(xl[:, (c + 1) % 2, :], g, c % 2, 1, xl_ready)
                g = s
                if live(g):
                    nc.gpsimd.tensor_scalar(neg_mask[:, :], adj_sb[:, c % 2, :], -1.0, NEG,
                                            ALU.add, ALU.mult).then_inc(neg_mask_ready, 1)

            run_steps(pool, step, -1, 6, 14, GROUPS + 3)

            def scale(g):
                nc.gpsimd.tensor_tensor(by_graph(group(xl_res, g)), by_graph(group(xl_res, g)),
                                        repeat(gamma_bc[:, :], G), ALU.mult).then_inc(scaled, 1)

            def shift(g):
                nc.gpsimd.tensor_tensor(by_graph(group(x_res, g)), by_graph(group(x_res, g)),
                                        repeat(beta_bc[:, :], G), ALU.add).then_inc(shifted, 1)

            def add(g):
                nc.gpsimd.tensor_tensor(group(x_res, g), group(x_res, g), group(xl_res, g),
                                        ALU.add).then_inc(final_ready, 1)

            def group_step(i, c):
                g = 2 * i + c
                if live(g) and not (isinstance(g, int) and g == 0):
                    wait(pool, bias2_in[c % 2], 16 * (i + (c + 1) // 2))
                    after(pool, bias2_in[c % 2], i, 16)
                    nc.gpsimd.tensor_tensor(group(xl_res, g), group(xl_res, g), group(b2bc, g),
                                            ALU.add).then_inc(res_ready, 1)
                if live(g):
                    shift(g)
                if live(g - 3):
                    wait(pool, unit_ready, g - 2)
                    after(pool, unit_ready, g)
                    scale(g - 3)
                    wait(pool, scaled, g - 2)
                    wait(pool, shifted, g - 2)
                    add(g - 3)

            pool.wait_ge(late_w_in, 16 * 5)
            for n in range(2):
                pool.wait_ge(xl_saved[n], 16 * (GROUPS // 2))
            run_steps(pool, group_step, 0, 4, GROUPS - 2, GROUPS + 2)

        @block.scalar
        def _(act):
            nc.scalar.preload_act_table_set("natural_log_exp_and_others")
            for n, src in enumerate((bq, bk, bv)):
                act.dma_start(bias_rows[n:n + 1, :], src.unsqueeze(0)).then_inc(rows_in, 16)
            act.dma_start(bias_rows[3:NROWS, :],
                          b1.rearrange("e (c p) -> (e c) p", p=P)).then_inc(rows_in, 16)

            def relu_of(dst, src, n, ready):
                nc.scalar.activation(dst[:, :], src[:, :], ACT.Relu,
                                     bias=bias_cols[:, n:n + 1]).then_inc(ready, 1)

            def exponentials(g, par):
                act.wait_ge(max_ready, g + 1)
                wait(act, probT_in_psum, g)
                wait(act, rden_ready, g - 1)
                for j in range(G):
                    last = nc.scalar.activation(
                        prob[:, j * P:(j + 1) * P], score[:, j * P:(j + 1) * P], ACT.Exp,
                        bias=neg_max[:, par, j:j + 1], accum_out=den[:, par, j:j + 1])
                last.then_inc(prob_ready, 1)

            def relu_y(g, par):
                act.wait_ge(y_in_psum, g + 1)
                act.wait_ge(rden_ready, g + 1)
                wait(act, x1_ready, g)
                for j in range(G):
                    last = nc.scalar.activation(rel[:, j * D:(j + 1) * D],
                                                b_y[:, j * D:(j + 1) * D], ACT.Relu,
                                                scale=rden[:, par, j:j + 1])
                last.then_inc(rel_ready, 1)

            def keep_xlT(g):
                act.wait_ge(xlT_in_psum, g + 1)
                nc.scalar.activation(group(xlT_res, g), b_t[:, :],
                                     ACT.Copy).then_inc(xlT_ready, 1)

            def step(i, c):
                s = 2 * i + c
                g = s
                if live(g):
                    act.wait_ge(xnT_in_psum, g + 1)
                    wait(act, v_in_psum, g)
                    nc.scalar.activation(xnT[:, :], b_t[:, :], ACT.Copy).then_inc(xnT_ready, 1)
                g = s - 2
                if live(g):
                    act.wait_ge(probT_in_psum, g + 1)
                    wait(act, y_in_psum, g)
                    nc.scalar.activation(probT[:, :], b_p[:, :], ACT.Copy).then_inc(probT_ready, 1)
                def guess_rstd():
                    lo, hi = ln_columns(s)
                    act.wait_ge(ln_chain, CHAIN1 * (s + 2) + 2)
                    wait(act, ln_ready, s + 2)
                    nc.scalar.activation(log_var[:, lo:hi], var_eps[:, lo:hi],
                                         ACT.Ln).then_inc(log_ready, 1)
                    act.wait_ge(log_ready, s + 3)
                    nc.scalar.activation(rough[:, lo:hi], log_var[:, lo:hi], ACT.Exp,
                                         scale=-0.5).then_inc(guess_ready, 1)

                if is_last(s - 3, GROUPS):
                    guess_rstd()
                if is_last(s - 2, GROUPS):
                    relu_y(s - 2, c % 2)
                elif live(s - 4):
                    keep_xlT(s - 4)
                if is_last(s - 1, GROUPS):
                    exponentials(s - 1, (c + 1) % 2)
                g = s
                if live(g):
                    act.wait_ge(q_in_psum, g + 1)
                    if isinstance(g, int) and g == 0:
                        act.wait_ge(cols_ready, 1)
                    wait(act, scores_in_psum, g)
                    relu_of(qT, b_q, 0, q_ready)
                if chained(s) and not is_last(s - 3, GROUPS):
                    guess_rstd()
                if live(g):
                    act.wait_ge(k_in_psum, g + 1)
                    relu_of(kT, b_k, 1, k_ready)
                if is_last(s - 2, GROUPS):
                    keep_xlT(s - 4)
                elif live(s - 2):
                    relu_y(s - 2, c % 2)
                g = s
                if live(g):
                    act.wait_ge(v_in_psum, g + 1)
                    wait(act, vw_in_psum, g)
                    relu_of(vT, b_v, 2, v_ready)
                if live(s - 1) and not is_last(s - 1, GROUPS):
                    exponentials(s - 1, (c + 1) % 2)

            run_steps(act, step, -2, 6, 12, GROUPS + 3)

            act.wait_ge(route_dve, 2)
            nc.scalar.activation(rt[:, 1, :], rt[:, 0, :], ACT.Exp, bias=r1[:, 0:1],
                                 accum_out=r1[:, 1:2]).then_inc(route_act, 1)
            keep_xlT(GROUPS - 1)
            act.wait_ge(route_dve, 8)
            nc.scalar.activation(rt[:, 5, :], rt[:, 4, :], ACT.Exp, bias=r1[:, 3:4],
                                 accum_out=r1[:, 4:5]).then_inc(route_act, 1)
            act.wait_ge(route_dve, 12)
            nc.scalar.activation(r1[:, 7:8], r1[:, 6:7], ACT.Exp,
                                 scale=r1[:, 5:6]).then_inc(route_act, 1)

            nc.scalar.preload_act_table(ACT.Gelu)

            def gelu(g, j):
                b = g * G + j
                act.wait_ge(h_in_psum, b + 1)
                wait(act, e_in_psum, b - G + 1)
                for k in range(TOP):
                    for f in range(FC):
                        at = (k * FC + f) * P
                        last = nc.scalar.activation(
                            hT[:, j, at:at + P], h_banks[j][:, at:at + P], ACT.Gelu,
                            bias=w1_pick[:, j, k, FF + f:FF + f + 1])
                last.then_inc(gelu_done, 1)

            def unit(g, j, at=0, end=G - 1):
                if j == 0:
                    wait(act, ln2_ready, g + 1)
                last = nc.scalar.activation(graph(xl_res, g * G + j), graph(xl_res, g * G + j),
                                            ACT.Identity, scale=rstd[:, at, j:j + 1],
                                            bias=neg_mr[:, at, j:j + 1])
                if j == end:
                    last.then_inc(unit_ready, 1)

            def group_step(g, gelus, units):
                for j in range(G):
                    if gelus:
                        gelu(g, j)
                    if units and j >= 2:
                        unit(g - 2, 2 * j - 4)
                        unit(g - 2, 2 * j - 3)

            group_step(0, True, False)
            group_step(1, True, False)
            with act.Fori(2, GROUPS) as g:
                group_step(g, True, True)
            nc.scalar.preload_act_table_set("natural_log_exp_and_others")
            group_step(GROUPS, False, True)
            act.wait_ge(ln2_chain, CHAIN2 * (GROUPS - 1) + 2)
            nc.scalar.activation(log_var[:, 0:G], var_eps[:, 0:G], ACT.Ln).then_inc(log_ready, 1)
            act.wait_ge(log_ready, GUESSES + 1)
            nc.scalar.activation(rough[:, 0:G], log_var[:, 0:G], ACT.Exp,
                                 scale=-0.5).then_inc(guess_ready, 1)
            for j in range(G // 2):
                unit(GROUPS - 1, j, 1, G // 2 - 1)

        @block.vector
        def _(dve):
            def rsqrt_op(n, chain, base, lo, hi, dst, ready):
                v, t, y = var_eps[:, lo:hi], newton_t[:, lo:hi], newton_y[:, lo:hi]
                dve.wait_ge(chain, base + n + 1)
                if n == 0:
                    op = nc.vector.tensor_scalar(halved[:, lo:hi], v.bitcast(I32), 1, None,
                                                 ALU.logical_shift_right)
                elif n == 1:
                    op = nc.vector.tensor_scalar(guess[:, lo:hi], halved[:, lo:hi], -1.0,
                                                 RSQRT_MAGIC, ALU.mult, ALU.add)
                else:
                    r, m = divmod(n - 2, 3)
                    prev = guess[:, lo:hi].bitcast(F32) if r == 0 else y
                    if m == 0:
                        op = nc.vector.tensor_tensor(t, prev, prev, ALU.mult)
                    elif m == 1:
                        op = nc.vector.scalar_tensor_tensor(t, t, -0.5, v, ALU.mult, ALU.mult)
                    else:
                        to = dst if r == NEWTONS - 1 else y
                        op = nc.vector.scalar_tensor_tensor(to, t, 1.5, prev, ALU.add, ALU.mult)
                op.then_inc(ready if n == 1 + 3 * NEWTONS else chain, 1)

            RSQRT_OPS = 2 + 3 * NEWTONS

            def bias_columns():
                dve.wait_ge(cols_in_psum, 1)
                nc.vector.tensor_copy(bias_cols[:, :], b_t[:, 0:3]).then_inc(cols_ready, 1)
                nc.vector.tensor_copy(w1v[:, :, FF:W1C],
                                      b_t[:, 3:NROWS].rearrange("p (e c) -> p e c", e=E)
                                      ).then_inc(cols_ready, 1)

            def step(i, c):
                s = 2 * i + c
                par, odd = c % 2, (c + 1) % 2

                def x_stats(js):
                    g = s + 3
                    if live(g):
                        for j in js:
                            op = nc.vector.bn_stats(stats[:, odd, j, :], graph(x_res, g * G + j))
                            if j == G - 1:
                                op.then_inc(stats1_done, 1)

                lo, hi = ln_columns(s)

                def refine(n):
                    if not chained(s):
                        return
                    y, t, v = rough[:, lo:hi], newton_t[:, lo:hi], var_eps[:, lo:hi]
                    if n == 0:
                        dve.wait_ge(guess_ready, s + 3)
                        nc.vector.tensor_tensor(t, y, y, ALU.mult).then_inc(ln_chain, 1)
                    elif n == 1:
                        dve.wait_ge(ln_chain, CHAIN1 * (s + 2) + 3)
                        nc.vector.scalar_tensor_tensor(t, t, -0.5, v, ALU.mult,
                                                       ALU.mult).then_inc(ln_chain, 1)
                    else:
                        dve.wait_ge(ln_chain, CHAIN1 * (s + 2) + 4)
                        nc.vector.scalar_tensor_tensor(rstd[:, par, lo:hi], t, 1.5, y, ALU.add,
                                                       ALU.mult).then_inc(ln_ready, 1)

                def mean_sums(g):
                    if is_last(g, GROUPS):
                        dve.wait_ge(mean_in_psum, 1)
                        nc.vector.tensor_copy(mean_sum[:, g * G:], b_w[:, 0:G]
                                              ).then_inc(mean_done, 1)
                    elif live(g):
                        dve.wait_ge(xlT_ready, g + 1)
                        nc.vector.tensor_reduce(mean_sum[:, bass.ds(g * G, G)],
                                                by_graph(group(xlT_res, g)),
                                                AX.X, ALU.add).then_inc(mean_done, 1)

                def row_max(ready, count):
                    wait(dve, prob_ready, s - 2)
                    dve.wait_ge(ready, count)
                    nc.vector.tensor_reduce(neg_max[:, odd, :], by_graph(score[:, :]), AX.X,
                                            ALU.max, negate=True).then_inc(max_ready, 1)

                def graph_layer_out(g):
                    dve.wait_ge(rel_ready, g + 1)
                    nc.vector.tensor_tensor(group(x_res, g), group(x_res, g), rel[:, :],
                                            ALU.add).then_inc(x1_ready, 1)
                    dve.wait_ge(x1_ready, g + 1)
                    for j in range(G):
                        op = nc.vector.bn_stats(stats[:, odd, G + j, :], graph(x_res, g * G + j))
                    op.then_inc(stats2_done, 1)

                draining = isinstance(s, int) and s >= GROUPS
                if isinstance(s, int) and s == -1:
                    bias_columns()
                g = s - 1
                if live(g):
                    dve.wait_ge(adj_in[odd], 16 * (i + (c - 1) // 2 + 1))
                    wait(dve, prob_ready, g)
                    dve.wait_ge(scores_in_psum, g + 1)
                    nc.vector.tensor_tensor(score[:, :], b_s[:, :], adj_sb[:, odd, :],
                                            ALU.mult).then_inc(scores_masked, 1)
                    if is_last(g, GROUPS):
                        dve.wait_ge(scores_masked, g + 1)
                        dve.wait_ge(neg_mask_ready, g + 1)
                        nc.vector.tensor_tensor(score[:, :], score[:, :], neg_mask[:, :],
                                                ALU.add).then_inc(last_score_ready, 1)
                        row_max(last_score_ready, 1)
                    wait(dve, y_in_psum, g - 1)
                    if isinstance(g, int) and g == 0:
                        dve.wait_ge(wo_in, 16 * 2)
                    dve.wait_ge(vw_in_psum, g + 1)
                    nc.vector.tensor_tensor(by_graph(vw[:, odd, :]), by_graph(b_w[:, :]),
                                            repeat(bo_bc[:, :], G), ALU.add).then_inc(vw_ready, 1)
                if live(s + 2):
                    dve.wait_ge(stats1_done, s + 3)
                    wait(dve, xn_ready, s + 1)
                if live(s - 3):
                    dve.wait_ge(stats2_done, s - 2)
                if chained(s):
                    wait(dve, xl_ready, s - 4)
                if live(s + 3):
                    dve.wait_ge(x_in[odd], 16 * (i + (c + 3) // 2 + 1))
                g = s - 2
                if live(g):
                    wait(dve, rel_ready, g - 1)
                    dve.wait_ge(prob_ready, g + 1)
                    nc.vector.reciprocal(rden[:, par, :], den[:, par, :]).then_inc(rden_ready, 1)
                if chained(s):
                    for j in range(lo, hi):
                        op = nc.vector.bn_aggr(mv[:, par, j, :], stats[:, par, j, :])
                    op.then_inc(ln_chain, 1)
                x_stats((0,))
                if chained(s):
                    dve.wait_ge(ln_chain, CHAIN1 * (s + 2) + 1)
                    nc.vector.tensor_scalar(var_eps[:, lo:hi], mv[:, par, lo:hi, 1], LN_EPS, None,
                                            ALU.add).then_inc(ln_chain, 1)
                    nc.vector.tensor_scalar(neg_mean[:, par, lo:hi], mv[:, par, lo:hi, 0], -1.0,
                                            None, ALU.mult)
                x_stats((1,))
                g = s - 1
                x_stats((2, 3))
                if not draining or is_last(s - 2, GROUPS):
                    mean_sums(s - 5)
                if is_last(s - 2, GROUPS):
                    graph_layer_out(s - 2)
                refine(0)
                if live(g) and not is_last(g, GROUPS):
                    row_max(score_ready, g + 1)
                refine(1)
                refine(2)
                if is_last(s - 3, GROUPS):
                    g = s - 3
                    dve.wait_ge(ln_ready, s + 3)
                    dve.wait_ge(xlT_in_psum, g - 1)
                    dve.wait_ge(xl_saved[odd], 16 * (g // 2))
                    for j in range(G):
                        op = nc.vector.tensor_scalar(
                            xl[:, odd, j * D:(j + 1) * D], graph(x_res, g * G + j),
                            neg_mean[:, par, G + j:G + j + 1], rstd[:, par, G + j:G + j + 1],
                            ALU.add, ALU.mult)
                    op.then_inc(last_xl_ready, 1)
                if draining and not is_last(s - 2, GROUPS):
                    mean_sums(s - 5)
                if live(s - 2) and not is_last(s - 2, GROUPS):
                    graph_layer_out(s - 2)

            run_steps(dve, step, -3, 6, 12, GROUPS + 5)

            count = [0]

            def then(op, needed=True):
                count[0] += 1
                op.then_inc(route_dve, 1)
                if needed:
                    dve.wait_ge(route_dve, count[0])

            def columns(n):
                return r1[:, n:n + 1]

            vec = nc.vector
            dve.wait_ge(route_pe, 1)
            dve.wait_ge(late_w_in, 16 * 5)
            then(vec.scalar_tensor_tensor(rt[:, 0, :], b_s[0:GRAPHS, 0:E], 1.0 / NODES,
                                          br_bc[:, :], ALU.mult, ALU.add))
            then(vec.tensor_reduce(columns(0), rt[:, 0, :], AX.X, ALU.max, negate=True))
            dve.wait_ge(route_act, 1)
            then(vec.reciprocal(columns(2), columns(1)))
            then(vec.tensor_scalar(rt[:, 2, :], rt[:, 1, :], columns(2), None, ALU.mult))
            dve.wait_ge(route_pe, 2)
            then(vec.reciprocal(rt[:, 6, :], b_s[0:GRAPHS, E:2 * E]))
            then(vec.tensor_scalar(rt[:, 7, :], rt[:, 6, :], CAPACITY / NODES, 1.0, ALU.mult,
                                   ALU.min))
            then(vec.tensor_tensor(rt[:, 4, :], rt[:, 2, :], rt[:, 7, :], ALU.mult))
            then(vec.tensor_reduce(columns(3), rt[:, 4, :], AX.X, ALU.max, negate=True))
            dve.wait_ge(route_act, 2)
            then(vec.max(rt[:, 9, :], rt[:, 5, :]))
            then(vec.max_index(top_at[:, :], rt[:, 9, :], rt[:, 5, :]), False)
            then(vec.reciprocal(columns(5), columns(4)), False)
            then(vec.tensor_tensor(columns(6), rt[:, 9, 1:2], rt[:, 9, 0:1], ALU.subtract))
            then(vec.tensor_copy(picked[:, TOP:2 * TOP], top_at[:, 0:TOP]))
            dve.wait_ge(const_ready, 2)
            dve.wait_ge(ident_ready, 1)

            def diagonal(lo):
                return vec.tensor_tensor(
                    picked_diag[:, lo:lo + TOP, :], repeat(ident[0:GRAPHS, 0:GRAPHS], TOP),
                    picked[:, lo:lo + TOP].unsqueeze(2).broadcast_to([GRAPHS, TOP, GRAPHS]),
                    ALU.mult)

            then(diagonal(TOP), False)
            dve.wait_ge(route_act, 3)
            then(vec.tensor_scalar(columns(8), columns(7), 1.0, None, ALU.add))
            then(vec.reciprocal(picked[:, 0:1], columns(8)))
            dve.wait_ge(route_pe, 3)
            for table, stride in ((w1_at, W1C), (w2_at, FC * D)):
                vec.tensor_scalar(table[:, :].rearrange("p (b k) -> p b k", k=TOP),
                                  b_w[0:1, 0:TOP * GRAPHS].rearrange("p (k b) -> p b k", k=TOP),
                                  float(stride), None, ALU.mult).then_inc(experts_ready, 1)
            then(vec.tensor_tensor(picked[:, 1:2], picked[:, 0:1], columns(7), ALU.mult))
            then(diagonal(0), False)
            for k in range(TOP):
                then(vec.tensor_scalar(rt[:, 10 + k, :], iota_e[:, :], picked[:, TOP + k:TOP + k + 1],
                                       picked[:, k:k + 1], ALU.is_equal, ALU.mult))
            then(vec.tensor_tensor(rt[:, 12, :], rt[:, 10, :], rt[:, 11, :], ALU.add), False)
            dve.wait_ge(route_pe, 4)
            vec.tensor_copy(w_bc[:, :, :], b_t[:, 0:TOP * GRAPHS]
                            .rearrange("p (k b) -> p k b", k=TOP)).then_inc(experts_ready, 1)
            dve.wait_ge(route_pe, 5)
            vec.tensor_copy(denseT[:, :], b_s[0:E, 0:GRAPHS]).then_inc(route_dve, 1)
            dve.wait_ge(w1_in, 16)
            dve.wait_ge(cols_ready, 2)

            def pick_places(first, graphs):
                return places(mybir.EngineType.DVE, w1_at, first, graphs, W1C)

            def pick(g, j, at):
                wait(dve, gelu_done, (g - 1) * G + j + 1)
                for k in range(TOP):
                    vec.tensor_copy(w1_pick[:, j, k, :],
                                    w1_sb[:, bass.ds(at[k], W1C)]
                                    ).then_inc(w1_picked, 1)

            at = pick_places(0, G - 1)
            pick(0, 0, at)
            dve.wait_ge(route_pe, 6)
            vec.tensor_copy(bias2[:, :], b_y[0:GRAPHS, 0:D]).then_inc(bias2_ready, 1)
            dve.wait_ge(first_res_in_psum, 1)
            for n in range(2):
                dve.wait_ge(xl_saved[n], 16 * (GROUPS // 2))
            vec.tensor_tensor(group(xl_res, 0), group(xl_res, 0), b_s[:, :], ALU.add
                              ).then_inc(first_res_ready, 1)
            for j in range(1, G - 1):
                pick(0, j, at[TOP * j:])
            dve.wait_ge(experts_ready, 3)

            def z_of(g, j, k):
                b = g * G + j
                by = y_banks[j]
                at = k * D
                if k == 0:
                    dve.wait_ge(e_in_psum, b + 1)
                    if j == 0:
                        if isinstance(g, int) and g == 0:
                            dve.wait_ge(first_res_ready, 1)
                        else:
                            dve.wait_ge(res_ready, g)
                else:
                    dve.wait_ge(z0_done, b + 1)
                vec.scalar_tensor_tensor(graph(xl_res, b), by[:, at:at + D],
                                         w_bc[:, k, bass.ds(b, 1)], graph(xl_res, b),
                                         ALU.mult, ALU.add).then_inc((z0_done, z_done)[k], 1)

            def z_stats(b, j):
                vec.bn_stats(stats[:, 0, j, :], graph(xl_res, b)).then_inc(zstats_done, 1)

            def aggregate(g):
                for j in range(G):
                    op = vec.bn_aggr(mv[:, 0, j, :], stats[:, 0, j, :])
                op.then_inc(ln2_chain, 1)

            def chain_op(g, n):
                base = CHAIN2 * g
                if n < 0:
                    dve.wait_ge(ln2_chain, base + 1)
                    vec.tensor_scalar(var_eps[:, 0:G], mv[:, 0, 0:G, 1], LN_EPS, None,
                                      ALU.add).then_inc(ln2_chain, 1)
                elif n < RSQRT_OPS:
                    if n == RSQRT_OPS - 1:
                        wait(dve, unit_ready, g)
                    rsqrt_op(n, ln2_chain, base + 1, 0, G, rstd[:, 0, 0:G], ln2_chain)
                else:
                    dve.wait_ge(ln2_chain, base + RSQRT_OPS + 2)
                    vec.scalar_tensor_tensor(neg_mr[:, 0, :], mv[:, 0, 0:G, 0], -1.0, rstd[:, 0, 0:G],
                                             ALU.mult, ALU.mult).then_inc(ln2_ready, 1)

            def group_step(g, zs, chain, picks, ops=3):
                if picks:
                    at = pick_places((g + 1) * G + 1, G - 2)
                if chain:
                    dve.wait_ge(zstats_done, g * G)
                n = -1
                for j in range(G):
                    if picks and 0 < j < G - 1:
                        pick(g + 1, j, at[TOP * (j - 1):])
                    if zs:
                        z_of(g, j, 0)
                    if chain and j == 0:
                        aggregate(g - 1)
                    if zs and j > 0:
                        dve.wait_ge(z_done, g * G + j)
                    if chain and n <= RSQRT_OPS:
                        chain_op(g - 1, n)
                    if zs and j > 0:
                        z_stats(g * G + j - 1, j - 1)
                    if chain and n < RSQRT_OPS:
                        chain_op(g - 1, n + 1)
                    if zs:
                        z_of(g, j, 1)
                    if chain:
                        for m in range(n + 2, min(n + ops, RSQRT_OPS + 1)):
                            chain_op(g - 1, m)
                    n += ops
                if zs:
                    dve.wait_ge(z_done, g * G + G)
                if chain:
                    for n in range(n, RSQRT_OPS + 1):
                        chain_op(g - 1, n)
                if zs:
                    z_stats(g * G + G - 1, G - 1)

            group_step(0, True, False, True)
            run_steps(dve, lambda i, c: group_step(2 * i + c, True, True, True), 1, 2, GROUPS - 2,
                      GROUPS - 1)
            g = GROUPS - 1
            group_step(g, True, True, False, 5)

            dve.wait_ge(zstats_done, GRAPHS)
            aggregate(g)
            dve.wait_ge(ln2_chain, CHAIN2 * g + 1)
            vec.tensor_scalar(var_eps[:, 0:G], mv[:, 0, 0:G, 1], LN_EPS, None,
                              ALU.add).then_inc(ln2_chain, 1)
            dve.wait_ge(guess_ready, GUESSES + 1)
            v, r, root = newton_t[:, 0:G], rough[:, 0:G], rstd[:, 1, 0:G]
            vec.tensor_tensor(v, r, r, ALU.mult).then_inc(ln2_chain, 1)
            dve.wait_ge(ln2_chain, CHAIN2 * g + 3)
            vec.scalar_tensor_tensor(v, v, -0.5, var_eps[:, 0:G], ALU.mult,
                                     ALU.mult).then_inc(ln2_chain, 1)
            dve.wait_ge(ln2_chain, CHAIN2 * g + 4)
            vec.scalar_tensor_tensor(root, v, 1.5, r, ALU.add, ALU.mult).then_inc(ln2_chain, 1)
            dve.wait_ge(ln2_chain, CHAIN2 * g + 5)
            vec.scalar_tensor_tensor(neg_mr[:, 1, :], mv[:, 0, 0:G, 0], -1.0, root,
                                     ALU.mult, ALU.mult).then_inc(ln2_ready, 1)
            dve.wait_ge(ln2_ready, GROUPS)
            for j in range(G // 2, G):
                op = vec.tensor_scalar(graph(xl_res, g * G + j), graph(xl_res, g * G + j),
                                       root[:, j:j + 1], neg_mr[:, 1, j:j + 1], ALU.mult, ALU.add)
            op.then_inc(last_unit, 1)
            for n in (1, 0):
                cut = slice((g * G + n * G // 2) * D, (g * G + (n + 1) * G // 2) * D)
                u = xl_res[:, cut].rearrange("p (g n) -> p g n", g=G // 2)
                if n == 0:
                    dve.wait_ge(unit_ready, GROUPS)
                else:
                    dve.wait_ge(last_unit, 1)
                vec.tensor_tensor(u, u, repeat(gamma_bc[:, :], G // 2), ALU.mult
                                  ).then_inc(last_scaled, 1)
                dve.wait_ge(last_scaled, 2 - n)
                dve.wait_ge(shifted, GROUPS)
                vec.tensor_tensor(x_res[:, cut], x_res[:, cut], xl_res[:, cut], ALU.add
                                  ).then_inc(last_final_ready, 1)

        @block.tensor
        def _(pe):
            def keep_busy(dst, times):
                for _ in range(times):
                    nc.tensor.matmul(dst[:, 0:2 * P], ones[:, 0:P], ones[:, 0:2 * P], start=True,
                                     stop=True)

            pe.wait_ge(const_ready, 1)
            keep_busy(b_p, WARM[0])
            pe.wait_ge(ident_ready, 1)
            pe.wait_ge(rows_in, 16 * 4)
            nc.tensor.transpose(b_t[:, 0:NROWS], bias_rows[:, :],
                                ident[0:NROWS, 0:NROWS]).then_inc(cols_in_psum, 1)
            pe.wait_ge(cols_ready, 2)
            pe.wait_ge(qkv_w_in, 16 * 3)

            def transposes(dst, src, done):
                for j in range(G):
                    op = nc.tensor.transpose(dst[:, j * P:(j + 1) * P], src[:, j * P:(j + 1) * P],
                                             ident[:, :])
                op.then_inc(done, 1)

            def products(dst, left, right, done):
                for j in range(G):
                    cut = slice(j * P, (j + 1) * P)
                    op = nc.tensor.matmul(dst[:, cut], left[:, cut],
                                          right[:, cut] if right.shape[-1] == GD else right,
                                          start=True, stop=True)
                op.then_inc(done, 1)

            def step(i, c):
                s = 2 * i + c
                g = s
                if live(g):
                    pe.wait_ge(xn_ready, g + 1)
                    wait(pe, xlT_ready, g - 4)
                    transposes(b_t, xn[:, c % 2, :], xnT_in_psum)
                g = s - 1
                if live(g):
                    pe.wait_ge(q_ready, g + 1)
                    pe.wait_ge(k_ready, g + 1)
                    wait(pe, scores_masked, g)
                    products(b_s, qT, kT, scores_in_psum)
                    if isinstance(g, int) and g == 0:
                        pe.wait_ge(wo_in, 16 * 2)
                    pe.wait_ge(v_ready, g + 1)
                    wait(pe, vw_ready, g)
                    products(b_w, vT, wo_sb[:, :], vw_in_psum)
                g = s - 2
                if is_last(g, GROUPS):
                    keep_busy(b_q, WARM[1])
                if live(g):
                    pe.wait_ge(prob_ready, g + 1)
                    wait(pe, probT_ready, g)
                    transposes(b_p, prob, probT_in_psum)
                def transpose_xl(g):
                    pe.wait_ge(xl_ready, g + 1)
                    if live(s):
                        wait(pe, xnT_ready, s + 1)
                    else:
                        wait(pe, xlT_ready, g)
                    transposes(b_t, xl[:, c % 2, :], xlT_in_psum)

                if live(s - 4) and not is_last(s - 4, GROUPS) and not is_last(s - 2, GROUPS):
                    transpose_xl(s - 4)

                def project(w, dst, done, free):
                    if live(s):
                        pe.wait_ge(xnT_ready, s + 1)
                        wait(pe, free, s)
                        nc.tensor.matmul(dst[:, :], w[:, :], xnT[:, :], start=True,
                                         stop=True).then_inc(done, 1)

                project(wq_sb, b_q, q_in_psum, q_ready)
                project(wk_sb, b_k, k_in_psum, k_ready)
                g = s - 2
                if live(g):
                    pe.wait_ge(probT_ready, g + 1)
                    pe.wait_ge(vw_ready, g + 1)
                    wait(pe, rel_ready, g)
                    products(b_y, probT, vw[:, c % 2, :], y_in_psum)
                if is_last(g, GROUPS):
                    transpose_xl(s - 4)
                project(wv_sb, b_v, v_in_psum, v_ready)
            run_steps(pe, step, 0, 6, 16, GROUPS + 2)
            keep_busy(b_p, WARM[2])
            step(0, GROUPS + 2)
            last_xl = xl[:, (GROUPS - 1) % 2, :]
            pe.wait_ge(last_xl_ready, 1)
            for j in range(G):
                op = nc.tensor.matmul(b_w[:, j:j + 1], last_xl[:, j * D:(j + 1) * D],
                                      ones[:, 0:1], start=True, stop=True)
            op.then_inc(mean_in_psum, 1)

            pe.wait_ge(mean_done, GROUPS)
            pe.wait_ge(late_w_in, 16 * 5)
            pe.wait_ge(const_ready, 2)
            nc.tensor.matmul(b_s[0:GRAPHS, 0:E], mean_sum[:, :], wr_sb[:, :], start=True,
                             stop=True).then_inc(route_pe, 1)
            pe.wait_ge(xlT_ready, GROUPS - 1)
            transposes(b_t, last_xl, xlT_in_psum)
            pe.wait_ge(route_dve, 4)
            nc.tensor.matmul(b_s[0:GRAPHS, E:2 * E], ones[0:GRAPHS, 0:GRAPHS], rt[:, 2, :],
                             start=True, stop=True).then_inc(route_pe, 1)
            keep_busy(b_p, WARM[3])

            def spread(dst, lo, step):
                pe.wait_ge(route_dve, step)
                nc.tensor.matmul(dst[:, 0:TOP * GRAPHS], ones[0:GRAPHS, 0:P],
                                 picked_diag[:, lo:lo + TOP, :].rearrange("b q c -> b (q c)"),
                                 start=True, stop=True).then_inc(route_pe, 1)

            spread(b_w, TOP, 14)
            keep_busy(b_p, WARM[4])
            spread(b_t, 0, 18)
            pe.wait_ge(route_dve, 21)
            nc.tensor.transpose(b_s[0:E, 0:GRAPHS], rt[:, 12, :],
                                ident[0:GRAPHS, 0:GRAPHS]).then_inc(route_pe, 1)
            keep_busy(b_p, WARM[5])
            pe.wait_ge(route_dve, 22)
            nc.tensor.matmul(b_y[0:GRAPHS, 0:D], denseT[:, :], b2_sb[:, :], start=True,
                             stop=True).then_inc(route_pe, 1)
            for j in range(G):
                op = nc.tensor.matmul(b_s[:, j * D:(j + 1) * D],
                                      denseT[:, j:j + 1].broadcast_to([E, P]), b2_sb[:, :],
                                      start=True, stop=True)
            op.then_inc(first_res_in_psum, 1)

            pe.wait_ge(w2_in, 16)
            pe.wait_ge(experts_ready, 2)
            pe.wait_ge(xlT_ready, GROUPS)

            def hidden(g, j):
                b = g * G + j
                if 0 < j < G - 1 or isinstance(g, int) and g == j == 0:
                    pe.wait_ge(w1_picked, TOP * (g * (G - 2) + j + 1))
                elif j == 0:
                    pe.wait_ge(w1_moved[0], 16 * TOP * g)
                else:
                    pe.wait_ge(w1_moved[1], 16 * TOP * (g + 1))
                wait(pe, gelu_done, b - G + 1)
                for k in range(TOP):
                    for f in range(FC):
                        at = (k * FC + f) * P
                        op = nc.tensor.matmul(h_banks[j][:, at:at + P],
                                              w1_pick[:, j, k, f * P:(f + 1) * P],
                                              graph(xlT_res, b), start=True, stop=True)
                op.then_inc(h_in_psum, 1)

            def experts(b, j, at):
                pe.wait_ge(gelu_done, b + 1)
                wait(pe, z_done, b - G + 1)
                for k in range(TOP):
                    for f in range(FC):
                        op = nc.tensor.matmul(y_banks[j][:, k * D:(k + 1) * D],
                                              hT[:, j, (k * FC + f) * P:(k * FC + f + 1) * P],
                                              w2_sb[:, bass.ds(at[k] + f * D, D)],
                                              start=(f == 0), stop=(f == FC - 1))
                op.then_inc(e_in_psum, 1)

            LAG = 2

            def group_step(g, lagging):
                first = 0 if lagging else LAG
                at = places(mybir.EngineType.PE, w2_at, g * G + first - LAG, G - first, FC * D)
                for j in range(G):
                    if not lagging and j == G - 1:
                        pe.wait_ge(experts_ready, 3)
                        pe.wait_ge(bias2_ready, 1)
                    hidden(g, j)
                    if j >= first:
                        n = TOP * (j - first)
                        if isinstance(g, int) and g == 1 and j == 0:
                            pe.wait_ge(first_res_ready, 1)
                        experts(g * G + j - LAG, (j - LAG) % G, at[n:n + TOP])

            group_step(0, False)
            group_step(1, True)
            with pe.Fori(2, GROUPS) as g:
                group_step(g, True)
            at = places(mybir.EngineType.PE, w2_at, GRAPHS - LAG, LAG, FC * D)
            for n in range(LAG):
                experts(GRAPHS - LAG + n, G - LAG + n, at[n * TOP:(n + 1) * TOP])


_INS = ["x", "adj", "L0_gnn_Wv", "L0_gnn_bv", "L0_gnn_Wk", "L0_gnn_bk", "L0_gnn_Wq", "L0_gnn_bq",
        "L0_gnn_Wo", "L0_gnn_bo", "L0_ffn_Wr", "L0_ffn_br", "L0_ffn_W1", "L0_ffn_b1", "L0_ffn_W2",
        "L0_ffn_b2", "L0_ffn_gamma", "L0_ffn_beta"]


def kernel(**inputs):
    import numpy as np
    import concourse.bacc as bacc
    from concourse.bass_utils import run_bass_kernel_spmd

    nc = bacc.Bacc("TRN2", target_bir_lowering=False, num_devices=1)
    arrays, args = {}, []
    for name in _INS:
        a = np.ascontiguousarray(inputs[name])
        arrays["in_" + name] = a
        args.append(nc.dram_tensor("in_" + name, a.shape, mybir.dt.from_np(a.dtype),
                                   kind="ExternalInput").ap())
    result = nc.dram_tensor("out_0", inputs["x"].shape, F32, kind="ExternalOutput").ap()
    build(nc, *args, result)
    r = run_bass_kernel_spmd(nc, [arrays], core_ids=[0])
    return r.results[0]["out_0"]
```
